# Optimizing a Trainium2 kernel written in Bass

```python
import numpy as np
import jax
import jax.numpy as jnp

def _softmax(x, axis=-1):
    return jax.nn.softmax(x, axis=axis)

def _gelu(x):
    return jax.nn.gelu(x, approximate=True)

def _silu(x):
    return jax.nn.silu(x)

def _sigmoid(x):
    return jax.nn.sigmoid(x)

def _layernorm(x, axis=-1, eps=1e-05):
    m = jnp.mean(x, axis=axis, keepdims=True)
    v = jnp.var(x, axis=axis, keepdims=True)
    return (x - m) / jnp.sqrt(v + eps)

def _scatter_add(tgt, idx, src, axis=0):
    return tgt.at[idx].add(src)

def _segment_sum(src, seg, n):
    return jax.ops.segment_sum(src, seg, n)
kernel_name = 'mk_xattn_ffn_d1_seqx_r8_d4f3e3'

def setup_inputs(seed: int=0):
    np.random.seed(seed)
    _w = jnp.asarray

    def _rec_inputs():
        import jax
        import jax.numpy as jnp
        _rk = jax.random.key(seed)
        x = -0.0003929 + 0.9999 * jax.random.normal(jax.random.fold_in(_rk, 1), (8, 56, 256), jnp.float32)
        _lenS = 56 - jax.random.randint(jax.random.fold_in(_rk, 7), (8,), 0, max(1, 56 // 4) + 1, jnp.int32)
        _lenS2 = 1500 - jax.random.randint(jax.random.fold_in(_rk, 8), (8,), 0, max(1, 1500 // 4) + 1, jnp.int32)
        _ctx_2048P = jax.random.normal(jax.random.fold_in(_rk, 11), (8, 16, 256), jnp.float32)
        _ctx_2048c = jax.random.dirichlet(jax.random.fold_in(_rk, 511), 0.3 * jnp.ones((16,), jnp.float32), (8, 1500))
        _ctx_2048t = jnp.einsum('bsk,bkd->bsd', _ctx_2048c, _ctx_2048P)
        _ctx_2048t = _ctx_2048t * jax.lax.rsqrt(jnp.mean(jnp.square(_ctx_2048t)) + 1e-12) * 0.953939
        ctx_2048 = -0.000514642 + 1.00011 * (_ctx_2048t + 0.3 * jax.random.normal(jax.random.fold_in(_rk, 611), (8, 1500, 256), jnp.float32))
        _validS = jnp.arange(56)[None, :] < _lenS[:, None]
        _validS2 = jnp.arange(1500)[None, :] < _lenS2[:, None]
        _causal = jnp.tril(jnp.ones((56, 56), dtype=bool))
        mask_BxS2_ik0 = jnp.where(jnp.broadcast_to(_validS2[:, :], (8, 1500)), 0, 1).astype(jnp.int32)
        return (x, ctx_2048, mask_BxS2_ik0)
    x, ctx_2048, mask_BxS2_ik0 = _rec_inputs()

    def _L0_xattn_setup():
        import jax, jax.numpy as jnp
        import numpy as np
        import math
        H = 256
        NH = 16
        HD = H // NH
        EPS_LN = 1e-05
        RES_SCALE_MAX = 0.3

        def _nan_clean(x, lim=10000.0):
            return jnp.nan_to_num(x, nan=0.0, posinf=lim, neginf=-lim)
        key = jax.random.key(seed)
        ks = jax.random.split(key, 12)
        B, S, T = (4, 256, 32)
        std = 1.0 / math.sqrt(H)
        return {'hidden_states': jax.random.normal(ks[0], (B, S, H), jnp.float32), 'audio_tokens': jax.random.normal(ks[1], (B, T, H), jnp.float32), 'attention_mask': jax.random.randint(ks[2], (B, T), 0, 2, jnp.int32), 'Wq': jax.random.normal(ks[3], (H, H), jnp.float32) * std, 'bq': jnp.zeros((H,), jnp.float32), 'Wk': jax.random.normal(ks[4], (H, H), jnp.float32) * std, 'bk': jnp.zeros((H,), jnp.float32), 'Wv': jax.random.normal(ks[5], (H, H), jnp.float32) * std, 'bv': jnp.zeros((H,), jnp.float32), 'Wo': jax.random.normal(ks[6], (H, H), jnp.float32) * std, 'bo': jnp.zeros((H,), jnp.float32), 'ln_gamma': jnp.ones((H,), jnp.float32), 'ln_beta': jnp.zeros((H,), jnp.float32), 'residual_scale': jnp.float32(0.05)}
    _L0_xattn_all = _L0_xattn_setup()
    _L0_xattn_in = {k: v for k, v in _L0_xattn_all.items() if k in ('Wq', 'bq', 'Wk', 'bk', 'Wv', 'bv', 'Wo', 'bo', 'ln_gamma', 'ln_beta', 'residual_scale')}
    del _L0_xattn_all

    def _L0_ffn_setup():
        import jax, jax.numpy as jnp
        import numpy as np
        E, K, H, F = (64, 6, 256, 96)
        G, KG = (8, 4)
        SHARED_F = 96
        SCALE = 2.5
        T = 2 * 128
        CAP = 2 * (T * K // E)

        def _grouped_topk(logits, bias):
            scores = jax.nn.sigmoid(logits.astype(jnp.float32))
            scores_b = scores + bias[None, :]
            gs = scores_b.reshape(-1, G, E // G)
            group_scores = jnp.sum(jax.lax.top_k(gs, 2)[0], axis=-1)
            gidx = jax.lax.top_k(group_scores, KG)[1]
            rows = jnp.arange(group_scores.shape[0])[:, None]
            group_mask = jnp.zeros_like(group_scores).at[rows, gidx].set(1.0)
            score_mask = jnp.repeat(group_mask, E // G, axis=-1) > 0
            tmp = jnp.where(score_mask, scores_b, -jnp.inf)
            topk_ids = jax.lax.top_k(tmp, K)[1]
            topk_w = jnp.take_along_axis(scores, topk_ids, axis=-1)
            topk_w = topk_w / jnp.sum(topk_w, axis=-1, keepdims=True)
            return (topk_w * SCALE, topk_ids)

        def _routed_moe(x, topk_w, topk_ids, w_gate, w_up, w_down):
            Tn = x.shape[0]
            flat_e = topk_ids.reshape(-1)
            order = jnp.argsort(flat_e)
            se = flat_e[order]
            pos = jnp.arange(Tn * K) - jnp.searchsorted(se, se, side='left')
            tok = order // K
            valid = pos < CAP
            slot = jnp.where(valid, pos, CAP)
            buf = jnp.zeros((E, CAP + 1, H), x.dtype).at[se, slot].set(x[tok])[:, :CAP]
            h = jax.nn.silu(jnp.einsum('ech,ehf->ecf', buf, w_gate)) * jnp.einsum('ech,ehf->ecf', buf, w_up)
            out = jnp.einsum('ecf,efh->ech', h, w_down)
            gathered = out[se, jnp.minimum(pos, CAP - 1)] * valid.astype(x.dtype)[:, None]
            w = topk_w.reshape(-1)[order].astype(x.dtype)[:, None]
            return jax.ops.segment_sum(gathered * w, tok, num_segments=Tn)
        key = jax.random.key(seed)
        ks = jax.random.split(key, 9)
        s = 0.02
        return dict(hidden_states=jax.random.normal(ks[0], (2, 128, H), jnp.float32), gate_w=jax.random.normal(ks[1], (H, E), jnp.float32) * s, bias=jax.random.normal(ks[2], (E,), jnp.float32) * s, w_gate=jax.random.normal(ks[3], (E, H, F), jnp.float32) * s, w_up=jax.random.normal(ks[4], (E, H, F), jnp.float32) * s, w_down=jax.random.normal(ks[5], (E, F, H), jnp.float32) * s, ws_gate=jax.random.normal(ks[6], (H, SHARED_F), jnp.float32) * s, ws_up=jax.random.normal(ks[7], (H, SHARED_F), jnp.float32) * s, ws_down=jax.random.normal(ks[8], (SHARED_F, H), jnp.float32) * s)
    _L0_ffn_all = _L0_ffn_setup()
    _L0_ffn_in = {k: v for k, v in _L0_ffn_all.items() if k in ('gate_w', 'bias', 'w_gate', 'w_up', 'w_down', 'ws_gate', 'ws_up', 'ws_down')}
    del _L0_ffn_all
    return {'x': x, 'ctx_2048': ctx_2048, 'mask_BxS2_ik0': mask_BxS2_ik0, 'L0_xattn_Wq': _L0_xattn_in['Wq'], 'L0_xattn_bq': _L0_xattn_in['bq'], 'L0_xattn_Wk': _L0_xattn_in['Wk'], 'L0_xattn_bk': _L0_xattn_in['bk'], 'L0_xattn_Wv': _L0_xattn_in['Wv'], 'L0_xattn_bv': _L0_xattn_in['bv'], 'L0_xattn_Wo': _L0_xattn_in['Wo'], 'L0_xattn_bo': _L0_xattn_in['bo'], 'L0_xattn_ln_gamma': _L0_xattn_in['ln_gamma'], 'L0_xattn_ln_beta': _L0_xattn_in['ln_beta'], 'L0_xattn_residual_scale': _L0_xattn_in['residual_scale'], 'L0_ffn_gate_w': _L0_ffn_in['gate_w'], 'L0_ffn_bias': _L0_ffn_in['bias'], 'L0_ffn_w_gate': _L0_ffn_in['w_gate'], 'L0_ffn_w_up': _L0_ffn_in['w_up'], 'L0_ffn_w_down': _L0_ffn_in['w_down'], 'L0_ffn_ws_gate': _L0_ffn_in['ws_gate'], 'L0_ffn_ws_up': _L0_ffn_in['ws_up'], 'L0_ffn_ws_down': _L0_ffn_in['ws_down']}

def reference(x, ctx_2048, mask_BxS2_ik0, L0_xattn_Wq, L0_xattn_bq, L0_xattn_Wk, L0_xattn_bk, L0_xattn_Wv, L0_xattn_bv, L0_xattn_Wo, L0_xattn_bo, L0_xattn_ln_gamma, L0_xattn_ln_beta, L0_xattn_residual_scale, L0_ffn_gate_w, L0_ffn_bias, L0_ffn_w_gate, L0_ffn_w_up, L0_ffn_w_down, L0_ffn_ws_gate, L0_ffn_ws_up, L0_ffn_ws_down):
    import jax
    import jax.numpy as jnp

    def _L0_xattn_ref(hidden_states, audio_tokens, attention_mask, Wq, bq, Wk, bk, Wv, bv, Wo, bo, ln_gamma, ln_beta, residual_scale):
        import jax, jax.numpy as jnp
        import numpy as np
        import math
        H = 256
        NH = 16
        HD = H // NH
        EPS_LN = 1e-05
        RES_SCALE_MAX = 0.3

        def _nan_clean(x, lim=10000.0):
            return jnp.nan_to_num(x, nan=0.0, posinf=lim, neginf=-lim)
        B, S, _ = hidden_states.shape
        T = audio_tokens.shape[1]
        hs = _nan_clean(hidden_states).astype(jnp.float32)
        at = _nan_clean(audio_tokens).astype(jnp.float32)

        def proj(x, W, b, L):
            y = x @ W.T + b
            return y.reshape(B, L, NH, HD).transpose(0, 2, 1, 3)
        q = _nan_clean(proj(hs, Wq, bq, S))
        k = _nan_clean(proj(at, Wk, bk, T))
        v = _nan_clean(proj(at, Wv, bv, T))
        scale = max(math.sqrt(HD), 1e-08)
        scores = jnp.einsum('bhsd,bhtd->bhst', q, k) / scale
        scores = jnp.clip(scores, -50.0, 50.0)
        scores = jnp.nan_to_num(scores, nan=0.0, posinf=50.0, neginf=-50.0)
        attend = (attention_mask.astype(jnp.float32) > 0.5)[:, None, None, :]
        scores = jnp.where(attend, scores, -10000.0)
        scores = jnp.clip(scores, -50.0, 50.0)
        probs = jax.nn.softmax(scores, axis=-1)
        probs = jnp.nan_to_num(probs, nan=0.0, posinf=1.0, neginf=0.0)
        probs = probs / (probs.sum(axis=-1, keepdims=True) + 1e-08)
        ctx = jnp.einsum('bhst,bhtd->bhsd', probs, v)
        ctx = ctx.transpose(0, 2, 1, 3).reshape(B, S, H)
        delta = _nan_clean(ctx @ Wo.T + bo)
        rs = jnp.clip(residual_scale, 0.0, RES_SCALE_MAX)
        delta = rs * delta
        mu = delta.mean(axis=-1, keepdims=True)
        var = jnp.mean((delta - mu) ** 2, axis=-1, keepdims=True)
        delta = (delta - mu) / jnp.sqrt(var + EPS_LN) * ln_gamma + ln_beta
        return delta

    def _L0_ffn_ref(hidden_states, gate_w, bias, w_gate, w_up, w_down, ws_gate, ws_up, ws_down):
        import jax, jax.numpy as jnp
        import numpy as np
        E, K, H, F = (64, 6, 256, 96)
        G, KG = (8, 4)
        SHARED_F = 96
        SCALE = 2.5
        T = 2 * 128
        CAP = 2 * (T * K // E)

        def _grouped_topk(logits, bias):
            scores = jax.nn.sigmoid(logits.astype(jnp.float32))
            scores_b = scores + bias[None, :]
            gs = scores_b.reshape(-1, G, E // G)
            group_scores = jnp.sum(jax.lax.top_k(gs, 2)[0], axis=-1)
            gidx = jax.lax.top_k(group_scores, KG)[1]
            rows = jnp.arange(group_scores.shape[0])[:, None]
            group_mask = jnp.zeros_like(group_scores).at[rows, gidx].set(1.0)
            score_mask = jnp.repeat(group_mask, E // G, axis=-1) > 0
            tmp = jnp.where(score_mask, scores_b, -jnp.inf)
            topk_ids = jax.lax.top_k(tmp, K)[1]
            topk_w = jnp.take_along_axis(scores, topk_ids, axis=-1)
            topk_w = topk_w / jnp.sum(topk_w, axis=-1, keepdims=True)
            return (topk_w * SCALE, topk_ids)

        def _routed_moe(x, topk_w, topk_ids, w_gate, w_up, w_down):
            Tn = x.shape[0]
            flat_e = topk_ids.reshape(-1)
            order = jnp.argsort(flat_e)
            se = flat_e[order]
            pos = jnp.arange(Tn * K) - jnp.searchsorted(se, se, side='left')
            tok = order // K
            valid = pos < CAP
            slot = jnp.where(valid, pos, CAP)
            buf = jnp.zeros((E, CAP + 1, H), x.dtype).at[se, slot].set(x[tok])[:, :CAP]
            h = jax.nn.silu(jnp.einsum('ech,ehf->ecf', buf, w_gate)) * jnp.einsum('ech,ehf->ecf', buf, w_up)
            out = jnp.einsum('ecf,efh->ech', h, w_down)
            gathered = out[se, jnp.minimum(pos, CAP - 1)] * valid.astype(x.dtype)[:, None]
            w = topk_w.reshape(-1)[order].astype(x.dtype)[:, None]
            return jax.ops.segment_sum(gathered * w, tok, num_segments=Tn)
        orig_shape = hidden_states.shape
        x = hidden_states.reshape(-1, H)
        router_logits = x @ gate_w
        topk_w, topk_ids = _grouped_topk(router_logits, bias)
        y = _routed_moe(x, topk_w, topk_ids, w_gate, w_up, w_down)
        shared = jax.nn.silu(x @ ws_gate) * (x @ ws_up) @ ws_down
        return (y + shared).reshape(orig_shape)
    x = x + _L0_xattn_ref(_layernorm(x, axis=-1), ctx_2048, mask_BxS2_ik0, L0_xattn_Wq, L0_xattn_bq, L0_xattn_Wk, L0_xattn_bk, L0_xattn_Wv, L0_xattn_bv, L0_xattn_Wo, L0_xattn_bo, L0_xattn_ln_gamma, L0_xattn_ln_beta, L0_xattn_residual_scale)
    x = x + _L0_ffn_ref(_layernorm(x, axis=-1), L0_ffn_gate_w, L0_ffn_bias, L0_ffn_w_gate, L0_ffn_w_up, L0_ffn_w_down, L0_ffn_ws_gate, L0_ffn_ws_up, L0_ffn_ws_down)
    return x

_drawn_inputs = setup_inputs


def setup_inputs(seed=0):
    import zlib

    import numpy as np

    out = dict(_drawn_inputs(seed))
    spreads = {'L0_xattn_bq': (0.0, 0.1),
     'L0_xattn_bk': (0.0, 0.8),
     'L0_xattn_bv': (0.0, 0.1),
     'L0_xattn_bo': (0.0, 0.1),
     'L0_xattn_ln_gamma': (1.0, 0.2),
     'L0_xattn_ln_beta': (0.0, 0.1)}
    factors = {'L0_ffn_gate_w': 8.0,
     'L0_ffn_bias': 8.0,
     'L0_ffn_w_gate': 8.0,
     'L0_ffn_w_up': 8.0,
     'L0_ffn_w_down': 8.0,
     'L0_ffn_ws_gate': 8.0,
     'L0_ffn_ws_up': 8.0,
     'L0_ffn_ws_down': 8.0}
    for name, (base, spread) in spreads.items():
        noise = np.random.default_rng([zlib.crc32(name.encode()), seed]).standard_normal(out[name].shape)
        drawn = base * np.exp(spread * noise) if base else spread * noise
        out[name] = jnp.asarray(drawn.astype(out[name].dtype))
    for name, factor in factors.items():
        out[name] = (out[name] * factor).astype(out[name].dtype)
    return out
```

```python
from contextlib import ExitStack

import concourse.bass as bass
from concourse import mybir

F32 = mybir.dt.float32
I32 = mybir.dt.int32
ALU = mybir.AluOpType
ACT = mybir.ActivationFunctionType
AX = mybir.AxisListType

B, S, H = 8, 56, 256
NH, HD = 16, 16
T = 1500
CH = 12
TP = T // CH
PARTS = 3
CPP = CH // PARTS
TOK = B * S
NT = 4
TT = TOK // NT
KH = 2
HPH = NH // KH
E, TOPK, F = 64, 6, 96
NG, TOPG = 8, 4
EPG = E // NG
CAP = 2 * (256 * TOPK // E)
SLOT = 64
SCALE = 2.5
GE = 4
GROUPS = E // GE
QUAD = 4
SW = 32
LIMIT = 10000.0
EXP_MIN, EXP_MAX = 1.9287498479639178e-22, 5.184705528587072e21
EPS = 1e-5
TOP_SENTINEL, TAKEN = 3.0e38, -3.0e38
HUGE = 1.0e30


def build(nc, x, ctx_in, mask_in, Wq, bq, Wk, bk, Wv, bv, Wo, bo, gamma, beta, rs, gate_w, rbias,
          w_gate, w_up, w_down, ws_gate, ws_up, ws_down, out):
    with ExitStack() as st:
        def sb(name, shape, dt=F32):
            return st.enter_context(nc.sbuf_tensor(name, shape, dt))

        def sem(name):
            return st.enter_context(nc.semaphore(name))

        PS = st.enter_context(nc.psum_tensor("PS", [128, 8, 512], F32))

        ident = sb("ident", [128, 128])
        head_mask = sb("head_mask", [128, HPH])
        before = sb("before", [TT, TT])
        ones = sb("ones", [TT, TT])
        slot_no = sb("slot_no", [TT, SLOT])
        x_sb = sb("x_sb", [TT, NT, H])
        w_raw = sb("w_raw", [128, 4, KH, H])
        bqk = sb("bqk", [128, 2, KH])
        bv_bc = sb("bv_bc", [128, H])
        bo_bc = sb("bo_bc", [TT, H])
        gamma_bc = sb("gamma_bc", [TT, H])
        beta_bc = sb("beta_bc", [TT, H])
        rbias_bc = sb("rbias_bc", [TT, E])
        rs_bc = sb("rs_bc", [TT, 1])
        mask_i = sb("mask_i", [TP, B, CH], I32)
        ctx_sb = sb("ctx_sb", [TP, PARTS, CPP, H])
        gate_sb = sb("gate_sb", [128, KH, E])
        sg_sb = sb("sg_sb", [128, KH, F])
        su_sb = sb("su_sb", [128, KH, F])
        sd_sb = sb("sd_sb", [F, H])
        wg_sb = sb("wg_sb", [128, QUAD, GE, KH, F])
        wu_sb = sb("wu_sb", [128, QUAD, GE, KH, F])
        wd_sb = sb("wd_sb", [F, QUAD, GE, H])
        wT = sb("wT", [128, 4, KH, H])
        attend = sb("attend", [TP, B, CH])
        sc_scale = sb("sc_scale", [TP, B, CH])
        sc_bias = sb("sc_bias", [TP, B, CH])
        stats = sb("stats", [TT, NT, 6])
        mv = sb("mv", [TT, NT, 2])
        std = sb("std", [TT, NT])
        rstd = sb("rstd", [TT, NT])
        xn = sb("xn", [TT, NT, H])
        xh = sb("xh", [TT, NT, H])
        clean_a = sb("clean_a", [128, NT * H])
        clean_m = sb("clean_m", [128, NT * H], I32)
        xT = sb("xT", [128, KH, TOK])
        q_raw = sb("q_raw", [128, KH, TOK])
        qT = sb("qT", [128, KH, TOK])
        q_bd = sb("q_bd", [128, B, KH, HPH, S])
        cT = sb("cT", [128, 2, KH, TP])
        kT = sb("kT", [128, 2, KH, TP])
        v_sb = sb("v_sb", [TP, 3, NH, SW])
        p_sb = sb("p_sb", [TP, 3, KH, HPH * S])
        o_all = sb("o_all", [128, NT, B, S])
        den = sb("den", [TT, NT * NH])
        rden = sb("rden", [TT, NT * NH])
        psum_p = sb("psum_p", [TT, NT * NH])
        ao = sb("ao", [TT, NT, H])
        delta = sb("delta", [TT, NT, H])
        x1 = sb("x1", [TT, NT, H])
        neg = sb("neg", [TT, NT, E])
        score = sb("score", [TT, NT, E])
        biased = sb("biased", [TT, NT, E])
        top_g = sb("top_g", [TT, NT, NG, 8])
        gsc = sb("gsc", [TT, NT, NG + 8])
        top8 = sb("top8", [TT, NT, 8])
        g_left = sb("g_left", [TT, NT, NG + 8])
        g_pick = sb("g_pick", [TT, NT, NG])
        g_off = sb("g_off", [TT, NT, NG])
        cand = sb("cand", [TT, NT, E + 8])
        e_left = sb("e_left", [TT, NT, E + 8])
        pick = sb("pick", [TT, NT, E])
        wsum = sb("wsum", [TT, NT])
        wtok = sb("wtok", [TT, NT, E])
        fits = sb("fits", [TT, NT, E])
        slot = sb("slot", [TT, NT, E])
        room = q_bd[:].rearrange("p b k h s -> p (b k h s)")
        used = [0]

        def again(parts, pattern, **dims):
            size = 1
            for d in dims.values():
                size *= d
            a = room[0:parts, used[0]:used[0] + size].rearrange(pattern, **dims)
            used[0] += size
            return a

        put = again(TT, "p (b i e s) -> p b i e s", b=2, i=NT, e=GE, s=SLOT)
        take = again(TT, "p (b i e s) -> p b i e s", b=2, i=NT, e=GE, s=SLOT)
        takeT = again(128, "p (b c t) -> p b c t", b=2, c=2, t=TOK)
        bufT = again(128, "p (b k s) -> p b k s", b=2, k=KH, s=GE * CAP)
        act_g = again(F, "p (b s) -> p b s", b=2, s=GE * CAP)
        hT = sb("hT", [F, 2, GE, SLOT])
        eo = sb("eo", [128, 2, 2, H])
        sh_g = sb("sh_g", [F, TOK])
        sh_h = sb("sh_h", [F, TOK])
        y_sb = sb("y_sb", [TT, NT, H])

        x_in, w_in, b_in, mask_in_s, small_in = sem("x_in"), sem("w_in"), sem("b_in"), sem("mask_in"), sem("small_in")
        ctx_loaded = [sem(f"ctx_loaded{j}") for j in range(PARTS)]
        ew_loaded = [sem(f"ew_loaded{j}") for j in range(QUAD)]
        out_done = sem("out_done")
        pool_step, consts, dve_step = sem("pool_step"), sem("consts"), sem("dve_step")
        var_ready, std_ready = sem("var_ready"), sem("std_ready")
        wT_psum, wT_ready = sem("wT_psum"), sem("wT_ready")
        xh_ready, xT_psum, xT_ready = sem("xh_ready"), sem("xT_psum"), sem("xT_ready")
        q_psum, qT_ready, qbd_ready, mask_ready = sem("q_psum"), sem("qT_ready"), sem("qbd_ready"), sem("mask_ready")
        cT_psum, cT_ready = sem("cT_psum"), sem("cT_ready")
        kv_psum, kT_ready, v_ready = sem("kv_psum"), sem("kT_ready"), sem("v_ready")
        s_psum, exp_done, p_ready, pv_done, o_saved = (sem("s_psum"), sem("exp_done"), sem("p_ready"),
                                                       sem("pv_done"), sem("o_saved"))
        oT_psum, ao_ready, aoT_psum, aoT_ready, od_psum = (sem("oT_psum"), sem("ao_ready"), sem("aoT_psum"),
                                                           sem("aoT_ready"), sem("od_psum"))
        logit_psum, neg_ready = sem("logit_psum"), sem("neg_ready")
        sh_psum, shg_ready, shh_ready = sem("sh_psum"), sem("shg_ready"), sem("shh_ready")
        pick_ready, pos_psum = sem("pick_ready"), sem("pos_psum")
        slot_ready = sem("slot_ready")
        put_ready, take_ready = sem("put_ready"), sem("take_ready")
        buf_psum, buf_ready = sem("buf_psum"), sem("buf_ready")
        gu_psum, actg_ready, h_ready = sem("gu_psum"), sem("actg_ready"), sem("h_ready")
        z_psum, z_saved = sem("z_psum"), sem("z_saved")
        combined = sem("combined")
        y_ready = sem("y_ready")

        block = st.enter_context(nc.Block())

        def turned_bank():
            return PS[:, 0, 0:KH * TP].rearrange("p (k t) -> p k t", k=KH)

        def key_bank(n):
            return PS[:, 1 + n % 2, 0:KH * TP].rearrange("p (k t) -> p k t", k=KH)

        def value_bank(n):
            return PS[0:TP, 1 + n % 2, 256:512]

        def score_banks(n):
            return PS[0:TP, 3 + 2 * (n % 2):5 + 2 * (n % 2), 0:HPH * S]

        def y_bank(i):
            return PS[0:TT, i // 2, (i % 2) * H:(i % 2 + 1) * H]

        def buf_bank(g):
            return PS[:, 2 + g % 2, 0:KH * GE * CAP].rearrange("p (k s) -> p k s", k=KH)

        def gu_bank(g, which):
            return PS[0:F, 4 + g % 2, which * GE * CAP:(which + 1) * GE * CAP]

        def after(eng, s, value):
            if isinstance(value, int) and value <= 0:
                return
            eng.wait_ge(s, value)

        ctx_v = ctx_in.rearrange("b (p c) d -> b p c d", c=CH)
        x_v = x.rearrange("b s d -> (b s) d").rearrange("(i p) d -> p i d", p=TT)
        out_v = out.rearrange("b s d -> (b s) d").rearrange("(i p) d -> p i d", p=TT)
        wg_v = w_gate.rearrange("e (p k) f -> p e k f", k=KH)
        wu_v = w_up.rearrange("e (p k) f -> p e k f", k=KH)
        wd_v = w_down.rearrange("e f d -> f e d")

        @block.sync
        def _(sp):
            def load_ctx(b, j):
                sp.dma_start(ctx_sb[:, j], ctx_v[b, :, j * CPP:(j + 1) * CPP, :]).then_inc(ctx_loaded[j], 16)

            def load_experts(g, c):
                sp.dma_start(wg_sb[:, c], wg_v[:, bass.ds(g * GE, GE)]).then_inc(ew_loaded[c], 16)
                sp.dma_start(wu_sb[:, c], wu_v[:, bass.ds(g * GE, GE)]).then_inc(ew_loaded[c], 16)
                sp.dma_start(wd_sb[:, c], wd_v[:, bass.ds(g * GE, GE)]).then_inc(ew_loaded[c], 16)

            sp.dma_start(x_sb[:], x_v).then_inc(x_in, 16)
            load_ctx(0, 0)
            for w, src in enumerate((Wq, Wk, Wv, Wo)):
                sp.dma_start(w_raw[:, w], src.rearrange("(o p) k -> p o k", p=128)).then_inc(w_in, 16)
            load_ctx(0, 1)
            load_ctx(0, 2)
            for c in range(QUAD):
                load_experts(c, c)

            with sp.Fori(1, B) as b:
                for j in range(PARTS):
                    sp.wait_ge(cT_psum, b * CH - CH + (j + 1) * CPP)
                    load_ctx(b, j)
            with sp.Fori(1, GROUPS // QUAD) as q:
                for c in range(QUAD):
                    sp.wait_ge(z_psum, (q * QUAD - QUAD + c + 1) * 3)
                    load_experts(q * QUAD + c, c)
            for i in range(2):
                sp.wait_ge(y_ready, i + 1)
                sp.dma_start(out_v[:, 2 * i:2 * i + 2], y_sb[:, 2 * i:2 * i + 2]).then_inc(out_done, 16)
            sp.wait_ge(out_done, 32)

        @block.gpsimd
        def _(pool):
            done = [0]

            def step(ins):
                done[0] += 1
                ins.then_inc(pool_step, 1)
                pool.wait_ge(pool_step, done[0])

            step(nc.gpsimd.memset(ident[:], 0.0))
            step(nc.gpsimd.affine_select(out=ident[:], in_=ident[:], compare_op=ALU.not_equal, fill=1.0, base=0,
                                         pattern=[[-1, 128]], channel_multiplier=1))
            step(nc.gpsimd.memset(head_mask[:], 1.0))
            step(nc.gpsimd.affine_select(out=head_mask[:], in_=head_mask[:], compare_op=ALU.is_ge, fill=0.0, base=0,
                                         pattern=[[-HD, HPH]], channel_multiplier=1))
            step(nc.gpsimd.affine_select(out=head_mask[:], in_=head_mask[:], compare_op=ALU.is_ge, fill=0.0,
                                         base=HD - 1, pattern=[[HD, HPH]], channel_multiplier=-1))
            step(nc.gpsimd.memset(v_sb[:], 1.0))
            step(nc.gpsimd.memset(hT[:], 0.0))
            step(nc.gpsimd.memset(ones[:], 1.0))
            step(nc.gpsimd.memset(before[:], 1.0))
            step(nc.gpsimd.affine_select(out=before[:], in_=before[:], compare_op=ALU.is_ge, fill=0.0, base=-1,
                                         pattern=[[1, TT]], channel_multiplier=-1))
            nc.gpsimd.iota(slot_no[:], pattern=[[1, SLOT]], base=0, channel_multiplier=0,
                           allow_small_or_imprecise_dtypes=True).then_inc(consts, 1)

            pool.wait_ge(qT_ready, 1)
            for b in range(B):
                nc.gpsimd.tensor_tensor(
                    q_bd[:, b], qT[:, :, b * S:(b + 1) * S].unsqueeze(2).to_broadcast([128, KH, HPH, S]),
                    head_mask[:].unsqueeze(1).unsqueeze(3).to_broadcast([128, KH, HPH, S]),
                    ALU.mult).then_inc(qbd_ready, 1)

            def weigh(g, c):
                pool.wait_ge(put_ready, g + 1)
                after(pool, z_psum, (g - 2) * 3 + 2)
                nc.gpsimd.tensor_tensor(
                    take[:, c % 2], put[:, c % 2],
                    wtok[:, :, bass.ds(g * GE, GE)].unsqueeze(3).to_broadcast([TT, NT, GE, SLOT]),
                    ALU.mult).then_inc(take_ready, 1)

            for c in range(QUAD):
                weigh(c, c)
            with pool.Fori(1, GROUPS // QUAD) as q:
                for c in range(QUAD):
                    weigh(q * QUAD + c, c)

        @block.scalar
        def _(act):
            act.dma_start(bqk[:, 0], bq.rearrange("(j p) -> p j", p=128), allow_slow_non_contiguous=True).then_inc(b_in, 16)
            act.dma_start(bqk[:, 1], bk.rearrange("(j p) -> p j", p=128), allow_slow_non_contiguous=True).then_inc(b_in, 16)
            act.dma_start(bv_bc[:], bv.partition_broadcast(128)).then_inc(b_in, 16)
            act.dma_start(mask_i[:], mask_in.rearrange("b (p c) -> p b c", c=CH)).then_inc(mask_in_s, 16)
            small = ((bo_bc, bo), (gamma_bc, gamma), (beta_bc, beta), (rbias_bc, rbias), (rs_bc, rs))
            for dst, src in small:
                act.dma_start(dst[:], src.partition_broadcast(TT)).then_inc(small_in, 16)
            act.dma_start(gate_sb[:], gate_w.rearrange("(k p) e -> p k e", p=128)).then_inc(small_in, 16)
            act.dma_start(sg_sb[:], ws_gate.rearrange("(k p) e -> p k e", p=128)).then_inc(small_in, 16)
            act.dma_start(su_sb[:], ws_up.rearrange("(k p) e -> p k e", p=128)).then_inc(small_in, 16)
            act.dma_start(sd_sb[:], ws_down).then_inc(small_in, 16)

            def root(n):
                act.wait_ge(var_ready, n)
                nc.scalar.activation(std[:], std[:], ACT.Sqrt).then_inc(std_ready, 1)

            root(1)
            for w in range(4):
                act.wait_ge(wT_psum, w + 1)
                nc.scalar.copy(wT[:, w], PS[:, w, :].rearrange("p (k o) -> p k o", k=KH)).then_inc(wT_ready, 1)
            act.wait_ge(xT_psum, 1)
            nc.scalar.copy(xT[:], PS[:, 4:6, 0:TOK]).then_inc(xT_ready, 1)
            act.wait_ge(mask_ready, 1)

            def turned(n, m):
                act.wait_ge(cT_psum, n + 1)
                after(act, kv_psum, n - 1)
                nc.scalar.copy(cT[:, m % 2], turned_bank()).then_inc(cT_ready, 1)

            def exps(n, b, c):
                act.wait_ge(s_psum, n + 1)
                after(act, pv_done, n - 2)
                nc.scalar.activation(p_sb[:, c % 3], score_banks(c), ACT.Exp, bias=sc_bias[:, b, c:c + 1],
                                     scale=sc_scale[:, b, c:c + 1]).then_inc(exp_done, 1)

            def batch(b, last):
                for c in range(CH):
                    exps(b * CH + c, b, c)
                    if c + 2 < CH or not last:
                        turned(b * CH + c + 2, c)

            turned(0, 0)
            turned(1, 1)
            batch(0, False)
            with act.Fori(1, B - 1) as b:
                batch(b, False)
            batch(B - 1, True)

            act.wait_ge(aoT_psum, 1)
            nc.scalar.copy(xT[:], PS[:, 4:6, 0:TOK]).then_inc(aoT_ready, 1)
            root(2)
            root(3)
            act.wait_ge(xT_psum, 2)
            nc.scalar.copy(xT[:], PS[:, 4:6, 0:TOK]).then_inc(xT_ready, 1)
            act.wait_ge(logit_psum, 1)
            nc.scalar.activation(neg[:], PS[0:TT, 6, 0:NT * E].rearrange("p (i e) -> p i e", i=NT), ACT.Exp,
                                 scale=-1.0).then_inc(neg_ready, 1)
            act.wait_ge(sh_psum, 1)
            nc.scalar.activation(sh_g[:], PS[0:F, 2, 0:TOK], ACT.Silu).then_inc(shg_ready, 1)

            def group(g, c):
                act.wait_ge(gu_psum, g + 1)
                after(act, h_ready, g - 1)
                nc.scalar.activation(act_g[:, c % 2], gu_bank(c, 0), ACT.Silu).then_inc(actg_ready, 1)
                after(act, combined, g - 1)
                for p in range(2):
                    act.wait_ge(z_psum, g * 3 + p + 1)
                    nc.scalar.copy(takeT[:, c % 2, p], PS[:, 6 + (3 * c + p) % 2, 0:TOK]).then_inc(z_saved, 1)
                act.wait_ge(z_psum, g * 3 + 3)
                nc.scalar.copy(eo[:, c % 2], PS[:, 6 + (3 * c + 2) % 2, :].rearrange("p (k d) -> p k d", k=2)).then_inc(z_saved, 1)

            for c in range(QUAD):
                group(c, c)
            with act.Fori(1, GROUPS // QUAD) as q:
                for c in range(QUAD):
                    group(q * QUAD + c, c)

        @block.vector
        def _(dve):
            done = [0]

            def step(ins):
                done[0] += 1
                ins.then_inc(dve_step, 1)
                dve.wait_ge(dve_step, done[0])

            def clean(dst, src, parts, cols):
                a, m = clean_a[0:parts, 0:cols], clean_m[0:parts, 0:cols]
                step(nc.vector.tensor_scalar(m, src, 0.0, 0.0, ALU.mult, ALU.is_equal))
                step(nc.vector.tensor_scalar(a, src, 0.0, LIMIT, ALU.max, ALU.min))
                step(nc.vector.tensor_scalar(dst, src, 0.0, -LIMIT, ALU.min, ALU.max))
                step(nc.vector.tensor_tensor(dst, dst, a, ALU.add))
                step(nc.vector.copy_predicated(dst, m, src))

            def layernorm(n, dst, src):
                for i in range(NT):
                    step(nc.vector.bn_stats(stats[:, i], src[:, i]))
                for i in range(NT):
                    step(nc.vector.bn_aggr(mv[:, i], stats[:, i]))
                nc.vector.tensor_scalar(std[:], mv[:, :, 1], EPS, None, ALU.add).then_inc(var_ready, 1)
                dve.wait_ge(std_ready, n)
                step(nc.vector.reciprocal(rstd[:], std[:]))
                for i in range(NT):
                    step(nc.vector.tensor_scalar(dst[:, i], src[:, i], mv[:, i, 0:1], rstd[:, i:i + 1],
                                                 ALU.subtract, ALU.mult))

            def flat(t):
                return t.rearrange("p i d -> p (i d)")

            dve.wait_ge(x_in, 16)
            layernorm(1, xn, x_sb)
            clean(flat(xh[:]), flat(xn[:]), TT, NT * H)
            nc.vector.memset(gsc[:, :, NG:], TOP_SENTINEL).then_inc(xh_ready, 1)
            step(nc.vector.memset(cand[:, :, E:], TOP_SENTINEL))
            dve.wait_ge(mask_in_s, 16)
            step(nc.vector.tensor_copy(attend[:], mask_i[:]))
            step(nc.vector.tensor_scalar(attend[:], attend[:], 0.5, None, ALU.is_gt))
            step(nc.vector.tensor_scalar(sc_scale[:], attend[:], 1.0 / HD ** 0.5, None, ALU.mult))
            nc.vector.tensor_scalar(sc_bias[:], attend[:], 50.0, -50.0, ALU.mult, ALU.add).then_inc(mask_ready, 1)
            dve.wait_ge(b_in, 48)
            dve.wait_ge(q_psum, 1)
            for j in range(KH):
                step(nc.vector.tensor_scalar(q_raw[:, j], PS[:, 6 + j, 0:TOK], bqk[:, 0, j:j + 1], None, ALU.add))
            clean(flat(qT[:]), flat(q_raw[:]), 128, KH * TOK)
            nc.vector.memset(den[:], 0.0).then_inc(qT_ready, 1)

            def keys(n, m):
                dve.wait_ge(kv_psum, n + 1)
                after(dve, s_psum, n - 1)
                nc.vector.tensor_tensor(kT[:, m % 2], key_bank(m), bqk[:, 1].unsqueeze(2).to_broadcast([128, KH, TP]),
                                        ALU.add).then_inc(kT_ready, 1)

            def values(n, m):
                after(dve, pv_done, n - 2)
                nc.vector.tensor_tensor(v_sb[:, m % 3, :, 0:HD], value_bank(m).rearrange("p (h d) -> p h d", h=NH),
                                        bv_bc[0:TP].rearrange("p (h d) -> p h d", h=NH), ALU.add).then_inc(v_ready, 1)

            def clip(n, c):
                dve.wait_ge(exp_done, n + 1)
                nc.vector.tensor_scalar(p_sb[:, c % 3], p_sb[:, c % 3], EXP_MIN, EXP_MAX, ALU.max, ALU.min).then_inc(p_ready, 1)

            def batch(b, last):
                for c in range(CH):
                    clip(b * CH + c, c)
                    if c + 1 < CH or not last:
                        keys(b * CH + c + 1, c + 1)
                        values(b * CH + c + 1, c + 1)
                dve.wait_ge(pv_done, b * CH + CH)
                nc.vector.tensor_copy(o_all[:, :, b, :], PS[:, 7, 0:NT * S].rearrange("p (g s) -> p g s", g=NT)).then_inc(o_saved, 1)

            dve.wait_ge(consts, 1)
            keys(0, 0)
            values(0, 0)
            batch(0, False)
            with dve.Fori(1, B - 1) as b:
                batch(b, False)
            batch(B - 1, True)

            dve.wait_ge(oT_psum, 1)
            heads = PS[0:TT, 0:4, :].rearrange("p b (h x) -> p (b h) x", x=SW)
            step(nc.vector.tensor_copy(den[:], heads[:, :, HD]))
            step(nc.vector.reciprocal(rden[:], den[:]))
            step(nc.vector.tensor_tensor(psum_p[:], den[:], rden[:], ALU.mult))
            step(nc.vector.tensor_scalar(psum_p[:], psum_p[:], 1e-8, None, ALU.add))
            step(nc.vector.reciprocal(psum_p[:], psum_p[:]))
            step(nc.vector.tensor_tensor(rden[:], rden[:], psum_p[:], ALU.mult))
            nc.vector.tensor_tensor(ao[:].rearrange("p i (h d) -> p (i h) d", d=HD), heads[:, :, 0:HD],
                                    rden[:].unsqueeze(2).to_broadcast([TT, NT * NH, HD]), ALU.mult).then_inc(ao_ready, 1)
            dve.wait_ge(small_in, 9 * 16)
            step(nc.vector.tensor_scalar(rs_bc[:], rs_bc[:], 0.0, 0.3, ALU.max, ALU.min))
            dve.wait_ge(od_psum, 1)
            for i in range(2):
                step(nc.vector.tensor_tensor(xn[:, 2 * i:2 * i + 2], PS[0:TT, 6 + i, :].rearrange("p (i d) -> p i d", i=2),
                                             bo_bc[:].unsqueeze(1).to_broadcast([TT, 2, H]), ALU.add))
            clean(flat(delta[:]), flat(xn[:]), TT, NT * H)
            step(nc.vector.tensor_scalar(flat(delta[:]), flat(delta[:]), rs_bc[:, 0:1], None, ALU.mult))
            layernorm(2, xn, delta)
            step(nc.vector.tensor_tensor(xn[:], xn[:], gamma_bc[:].unsqueeze(1).to_broadcast([TT, NT, H]), ALU.mult))
            step(nc.vector.tensor_tensor(xn[:], xn[:], beta_bc[:].unsqueeze(1).to_broadcast([TT, NT, H]), ALU.add))
            step(nc.vector.tensor_tensor(x1[:], x_sb[:], xn[:], ALU.add))
            layernorm(3, xn, x1)
            nc.vector.memset(den[:], 0.0).then_inc(xh_ready, 1)

            dve.wait_ge(neg_ready, 1)
            step(nc.vector.tensor_scalar(neg[:], neg[:], 1.0, None, ALU.add))
            step(nc.vector.reciprocal(score[:], neg[:]))
            step(nc.vector.tensor_tensor(biased[:], score[:], rbias_bc[:].unsqueeze(1).to_broadcast([TT, NT, E]), ALU.add))
            for i in range(NT):
                for k in range(NG):
                    ins = nc.vector.max(top_g[:, i, k], biased[:, i, k * EPG:(k + 1) * EPG])
                step(ins)
            step(nc.vector.tensor_tensor(gsc[:, :, 0:NG], top_g[:, :, :, 0], top_g[:, :, :, 1], ALU.add))

            def first_best(values, best, left, width, count):
                for i in range(NT):
                    step(nc.vector.max(best[:, i], values[:, i, 0:width]))
                step(nc.vector.memset(best[:, :, count:8], TOP_SENTINEL))
                for i in range(NT):
                    step(nc.vector.match_replace(left[:, i], best[:, i], values[:, i], TAKEN))

            first_best(gsc, top8, g_left, NG, TOPG)
            step(nc.vector.tensor_scalar(g_pick[:], g_left[:, :, 0:NG], TAKEN, None, ALU.is_equal))
            step(nc.vector.tensor_scalar(g_off[:], g_pick[:], HUGE, -HUGE, ALU.mult, ALU.add))
            cand_g = cand[:, :, 0:E].rearrange("p i (k e) -> p i k e", k=NG)
            step(nc.vector.tensor_tensor(cand_g, biased[:].rearrange("p i (k e) -> p i k e", k=NG),
                                         g_pick[:].unsqueeze(3).to_broadcast([TT, NT, NG, EPG]), ALU.mult))
            step(nc.vector.tensor_tensor(cand_g, cand_g, g_off[:].unsqueeze(3).to_broadcast([TT, NT, NG, EPG]), ALU.add))
            first_best(cand, top8, e_left, E, TOPK)
            step(nc.vector.tensor_scalar(pick[:], e_left[:, :, 0:E], TAKEN, None, ALU.is_equal))
            nc.vector.tensor_tensor(wtok[:], score[:], pick[:], ALU.mult).then_inc(pick_ready, 1)
            dve.wait_ge(pick_ready, 1)
            step(nc.vector.tensor_reduce(wsum[:], wtok[:], AX.X, ALU.add))
            step(nc.vector.reciprocal(wsum[:], wsum[:]))
            step(nc.vector.tensor_tensor(wtok[:], wtok[:], wsum[:].unsqueeze(2).to_broadcast([TT, NT, E]), ALU.mult))
            step(nc.vector.tensor_scalar(wtok[:], wtok[:], SCALE, None, ALU.mult))
            dve.wait_ge(pos_psum, 1)
            pos = PS[0:TT, 7, 0:NT * E].rearrange("p (i e) -> p i e", i=NT)
            step(nc.vector.tensor_scalar(fits[:], pos, float(CAP), None, ALU.is_lt))
            step(nc.vector.tensor_tensor(fits[:], fits[:], pick[:], ALU.mult))
            step(nc.vector.tensor_scalar(slot[:], pos, 1.0, None, ALU.add))
            step(nc.vector.tensor_tensor(slot[:], slot[:], fits[:], ALU.mult))
            step(nc.vector.tensor_scalar(slot[:], slot[:], -1.0, None, ALU.add))
            dve.wait_ge(shg_ready, 1)
            nc.vector.tensor_tensor(sh_h[:], sh_g[:], PS[0:F, 3, 0:TOK], ALU.mult).then_inc(shh_ready, 1)

            def routes(g, c):
                after(dve, buf_psum, g - 1)
                after(dve, take_ready, g - 1)
                nc.vector.tensor_tensor(
                    put[:, c % 2], slot_no[:].unsqueeze(1).unsqueeze(1).to_broadcast([TT, NT, GE, SLOT]),
                    slot[:, :, bass.ds(g * GE, GE)].unsqueeze(3).to_broadcast([TT, NT, GE, SLOT]),
                    ALU.is_equal).then_inc(put_ready, 1)

            def gathered(g, c):
                dve.wait_ge(buf_psum, g + 1)
                after(dve, gu_psum, g - 1)
                nc.vector.tensor_copy(bufT[:, c % 2], buf_bank(c)).then_inc(buf_ready, 1)

            def hidden(g, c):
                dve.wait_ge(actg_ready, g + 1)
                after(dve, z_psum, (g - 1) * 3)
                nc.vector.tensor_tensor(hT[:, c % 2, :, 0:CAP], act_g[:, c % 2].rearrange("f (e s) -> f e s", e=GE),
                                        gu_bank(c, 1).rearrange("f (e s) -> f e s", e=GE), ALU.mult).then_inc(h_ready, 1)

            def quad(q):
                for c in range(QUAD):
                    g = q * QUAD + c
                    if c == 0:
                        routes(g, c)
                        gathered(g, c)
                    if c + 1 < QUAD:
                        routes(g + 1, c + 1)
                    hidden(g, c)
                    if c + 1 < QUAD:
                        gathered(g + 1, c + 1)

            quad(0)
            with dve.Fori(1, GROUPS // QUAD) as q:
                quad(q)

            dve.wait_ge(combined, GROUPS)
            for i in range(2):
                nc.vector.tensor_tensor(y_sb[:, 2 * i:2 * i + 2], PS[0:TT, i, :].rearrange("p (i d) -> p i d", i=2),
                                        x1[:, 2 * i:2 * i + 2], ALU.add).then_inc(y_ready, 1)

        @block.tensor
        def _(pe):
            mm, turn = nc.tensor.matmul, nc.tensor.transpose

            pe.wait_ge(consts, 1)
            for w in range(4):
                if w == 0:
                    pe.wait_ge(w_in, 64)
                for k in range(KH):
                    for o in range(KH):
                        ins = turn(PS[:, w, k * H + o * 128:k * H + o * 128 + 128], w_raw[:, w, o, k * 128:k * 128 + 128], ident[:])
                ins.then_inc(wT_psum, 1)

            def turn_tokens(src, s):
                for k in range(KH):
                    for i in range(NT):
                        ins = turn(PS[:, 4 + k, i * TT:(i + 1) * TT], src[:, i, k * 128:(k + 1) * 128], ident[0:TT, 0:TT])
                ins.then_inc(s, 1)

            pe.wait_ge(xh_ready, 1)
            turn_tokens(xh, xT_psum)
            pe.wait_ge(xT_ready, 1)
            pe.wait_ge(wT_ready, 4)
            for j in range(KH):
                for k in range(KH):
                    ins = mm(PS[:, 6 + j, 0:TOK], wT[:, 0, k, j * 128:(j + 1) * 128], xT[:, k, :], start=(k == 0), stop=(k == KH - 1))
            ins.then_inc(q_psum, 1)

            def turned(n, m, b):
                after(pe, cT_ready, n)
                if m % CPP == 0:
                    pe.wait_ge(ctx_loaded[m // CPP], (b + 1) * 16)
                for k in range(KH):
                    ins = turn(turned_bank()[:, k, :], ctx_sb[:, m // CPP, m % CPP, k * 128:(k + 1) * 128], ident[0:TP, 0:TP])
                ins.then_inc(cT_psum, 1)

            def project(n, m):
                pe.wait_ge(cT_ready, n + 1)
                after(pe, kT_ready, n - 1)
                after(pe, v_ready, n - 1)
                for j in range(KH):
                    for k in range(KH):
                        mm(key_bank(m)[:, j, :], wT[:, 1, k, j * 128:(j + 1) * 128], cT[:, m % 2, k, :],
                           start=(k == 0), stop=(k == KH - 1))
                for k in range(KH):
                    ins = mm(value_bank(m), cT[:, m % 2, k, :], wT[:, 2, k, :], start=(k == 0), stop=(k == KH - 1))
                ins.then_inc(kv_psum, 1)

            def scores(n, m, b):
                pe.wait_ge(kT_ready, n + 1)
                after(pe, exp_done, n - 1)
                for j in range(KH):
                    ins = mm(score_banks(m)[:, j, :], kT[:, m % 2, j, :], q_bd[:, b, j].rearrange("p h s -> p (h s)"),
                             start=True, stop=True)
                ins.then_inc(s_psum, 1)

            def weigh_values(n, m):
                pe.wait_ge(p_ready, n + 1)
                for h in range(NH):
                    i, g = h % NT, h // NT
                    ins = mm(PS[32 * i:32 * i + SW, 7, g * S:(g + 1) * S], v_sb[:, m % 3, h, :],
                             p_sb[:, m % 3, h // HPH, (h % HPH) * S:(h % HPH + 1) * S],
                             start=(m == 0 and g == 0), stop=(m == CH - 1), skip_group_check=True)
                ins.then_inc(pv_done, 1)

            def batch(b, last):
                for c in range(CH):
                    n = b * CH + c
                    if c == 0:
                        pe.wait_ge(qbd_ready, b + 1)
                    scores(n, c, b)
                    if c + 2 < CH or not last:
                        turned(n + 2, (c + 2) % CH, b + (c + 2) // CH)
                    if c + 1 < CH or not last:
                        project(n + 1, c + 1)
                    if c == 1:
                        after(pe, o_saved, b)
                    if c >= 1:
                        weigh_values(n - 1, c - 1)
                weigh_values(b * CH + CH - 1, CH - 1)

            turned(0, 0, 0)
            turned(1, 1, 0)
            project(0, 0)
            batch(0, False)
            with pe.Fori(1, B - 1) as b:
                batch(b, False)
            batch(B - 1, True)

            pe.wait_ge(o_saved, B)
            for i in range(NT):
                for g in range(NT):
                    ins = turn(PS[0:TT, i, g * 128:(g + 1) * 128], o_all[:, g, 2 * i:2 * i + 2, :].rearrange("p b s -> p (b s)"), ident[:])
            ins.then_inc(oT_psum, 1)
            pe.wait_ge(ao_ready, 1)
            turn_tokens(ao, aoT_psum)
            pe.wait_ge(aoT_ready, 1)
            for i in range(NT):
                for k in range(KH):
                    ins = mm(PS[0:TT, 6 + i // 2, (i % 2) * H:(i % 2 + 1) * H], xT[:, k, i * TT:(i + 1) * TT], wT[:, 3, k, :],
                             start=(k == 0), stop=(k == KH - 1))
            ins.then_inc(od_psum, 1)

            pe.wait_ge(xh_ready, 2)
            turn_tokens(xn, xT_psum)
            pe.wait_ge(xT_ready, 2)
            for i in range(NT):
                for k in range(KH):
                    ins = mm(PS[0:TT, 6, i * E:(i + 1) * E], xT[:, k, i * TT:(i + 1) * TT], gate_sb[:, k, :],
                             start=(k == 0), stop=(k == KH - 1))
            ins.then_inc(logit_psum, 1)
            for u, w in enumerate((sg_sb, su_sb)):
                for k in range(KH):
                    ins = mm(PS[0:F, 2 + u, 0:TOK], w[:, k, :], xT[:, k, :], start=(k == 0), stop=(k == KH - 1))
            ins.then_inc(sh_psum, 1)
            pe.wait_ge(pick_ready, 1)
            for i in range(NT):
                for j in range(i + 1):
                    ins = mm(PS[0:TT, 7, i * E:(i + 1) * E], before[:] if j == i else ones[:], pick[:, j, :],
                             start=(j == 0), stop=(j == i))
            ins.then_inc(pos_psum, 1)
            pe.wait_ge(shh_ready, 1)
            for i in range(NT):
                mm(y_bank(i), sh_h[:, i * TT:(i + 1) * TT], sd_sb[:], start=(i % 2 == 0), stop=False, skip_group_check=True)

            def gather(g, c):
                pe.wait_ge(put_ready, g + 1)
                after(pe, buf_ready, g - 1)
                for k in range(KH):
                    for i in range(NT):
                        ins = mm(buf_bank(c)[:, k, :], xn[:, i, k:H:KH], put[:, c % 2, i, :, 0:CAP], start=(i == 0), stop=(i == NT - 1))
                ins.then_inc(buf_psum, 1)

            def gate_up(g, c, q):
                pe.wait_ge(buf_ready, g + 1)
                pe.wait_ge(ew_loaded[c], (q + 1) * 48)
                after(pe, h_ready, g - 1)
                for u, w in enumerate((wg_sb, wu_sb)):
                    for e in range(GE):
                        for k in range(KH):
                            ins = mm(gu_bank(c, u)[:, e * CAP:(e + 1) * CAP], w[:, c, e, k, :],
                                     bufT[:, c % 2, k, e * CAP:(e + 1) * CAP], start=(k == 0), stop=(k == KH - 1))
                ins.then_inc(gu_psum, 1)

            def turn_take(g, c):
                pe.wait_ge(take_ready, g + 1)
                for p in range(2):
                    z = 3 * c + p
                    after(pe, z_saved, g * 3 + p - 1)
                    for i in range(NT):
                        ins = turn(PS[:, 6 + z % 2, i * TT:(i + 1) * TT],
                                   take[:, c % 2, i, 2 * p:2 * p + 2, :].rearrange("t e s -> t (e s)"), ident[0:TT, 0:TT])
                    ins.then_inc(z_psum, 1)

            def down(g, c):
                pe.wait_ge(h_ready, g + 1)
                after(pe, z_saved, g * 3 + 1)
                z = 3 * c + 2
                for e in range(GE):
                    r = 64 * (e % 2)
                    ins = mm(PS[r:r + SLOT, 6 + z % 2, (e // 2) * H:(e // 2 + 1) * H], hT[:, c % 2, e, :], wd_sb[:, c, e, :],
                             start=True, stop=True, skip_group_check=True)
                ins.then_inc(z_psum, 1)

            def combine(g, c):
                pe.wait_ge(z_saved, g * 3 + 3)
                for p in range(2):
                    for i in range(NT):
                        ins = mm(y_bank(i), takeT[:, c % 2, p, i * TT:(i + 1) * TT], eo[:, c % 2, p, :],
                                 start=False, stop=True, skip_group_check=True)
                ins.then_inc(combined, 1)

            def quad(q):
                for c in range(QUAD):
                    g = q * QUAD + c
                    if c == 0:
                        gather(g, c)
                    gate_up(g, c, q)
                    turn_take(g, c)
                    if c + 1 < QUAD:
                        gather(g + 1, c + 1)
                    if c > 0:
                        combine(g - 1, c - 1)
                    down(g, c)
                combine(q * QUAD + QUAD - 1, QUAD - 1)

            quad(0)
            with pe.Fori(1, GROUPS // QUAD) as q:
                quad(q)


_INS = ["x", "ctx_2048", "mask_BxS2_ik0", "L0_xattn_Wq", "L0_xattn_bq", "L0_xattn_Wk", "L0_xattn_bk", "L0_xattn_Wv",
        "L0_xattn_bv", "L0_xattn_Wo", "L0_xattn_bo", "L0_xattn_ln_gamma", "L0_xattn_ln_beta",
        "L0_xattn_residual_scale", "L0_ffn_gate_w", "L0_ffn_bias", "L0_ffn_w_gate", "L0_ffn_w_up", "L0_ffn_w_down",
        "L0_ffn_ws_gate", "L0_ffn_ws_up", "L0_ffn_ws_down"]


def kernel(**inputs):
    import numpy as np
    import concourse.bacc as bacc
    from concourse.bass_utils import run_bass_kernel_spmd

    nc = bacc.Bacc("TRN2", target_bir_lowering=False, num_devices=1)
    arrays, args = {}, []
    for name in _INS:
        a = np.ascontiguousarray(inputs[name])
        if a.ndim == 0:
            a = a.reshape(1)
        arrays[f"in_{name}"] = a
        args.append(nc.dram_tensor(f"in_{name}", a.shape, mybir.dt.from_np(a.dtype), kind="ExternalInput").ap())
    args.append(nc.dram_tensor("out_0", (B, S, H), F32, kind="ExternalOutput").ap())
    build(nc, *args)
    r = run_bass_kernel_spmd(nc, [arrays], core_ids=[0])
    return r.results[0]["out_0"]
```

```python
from contextlib import ExitStack

import concourse.bass as bass
from concourse import mybir

F32 = mybir.dt.float32
I32 = mybir.dt.int32
BF16 = mybir.dt.bfloat16
F32R = mybir.dt.float32r
ALU = mybir.AluOpType
ACT = mybir.ActivationFunctionType
AX = mybir.AxisListType

B, S, H = 8, 56, 256
NH, HD = 16, 16
T = 1500
CH = 12
PAIRS = CH // 2
TP = T // CH
TPE = TP + TP % 2
PARTS = 3
CPP = CH // PARTS
TOK = B * S
NT = 4
TT = TOK // NT
KH = 2
HPH = NH // KH
E, TOPK, F = 64, 6, 96
NG, TOPG = 8, 4
EPG = E // NG
CAP = 2 * (256 * TOPK // E)
SLOT = 64
SCALE = 2.5
GE = 4
GROUPS = E // GE
QUAD = 4
SW = 32
LIMIT = 10000.0
EXP_MIN, EXP_MAX = 1.9287498479639178e-22, 5.184705528587072e21
EPS = 1e-5
TOP_SENTINEL, TAKEN = 3.0e38, -3.0e38
HUGE = 1.0e30


def build(nc, x, ctx_in, mask_in, Wq, bq, Wk, bk, Wv, bv, Wo, bo, gamma, beta, rs, gate_w, rbias,
          w_gate, w_up, w_down, ws_gate, ws_up, ws_down, out):
    with ExitStack() as st:
        def sb(name, shape, dt=F32):
            return st.enter_context(nc.sbuf_tensor(name, shape, dt))

        def sem(name):
            return st.enter_context(nc.semaphore(name))

        PS = st.enter_context(nc.psum_tensor("PS", [128, 8, 512], F32))

        ident = sb("ident", [128, 128])
        ident_b = sb("ident_b", [128, 128], BF16)
        head_mask = sb("head_mask", [128, HPH])
        before = sb("before", [TT, TT])
        ones = sb("ones", [TT, TT])
        slot_no = sb("slot_no", [TT, SLOT])
        x_sb = sb("x_sb", [TT, NT, H])
        w_raw = sb("w_raw", [128, 4, KH, H])
        bqk = sb("bqk", [128, 2, KH])
        bv_bc = sb("bv_bc", [128, H])
        bo_bc = sb("bo_bc", [TT, H])
        gamma_bc = sb("gamma_bc", [TT, H])
        beta_bc = sb("beta_bc", [TT, H])
        rbias_bc = sb("rbias_bc", [TT, E])
        rs_bc = sb("rs_bc", [TT, 1])
        mask_i = sb("mask_i", [TP, B, CH], I32)
        room = sb("room", [128, PARTS * CPP * H + 3 * NH * S + 4 * NH * SW])
        room_r = sb("room_r", [128, 2 * NT * H + 2 * NT * GE * SLOT + 4 * TOK + 8 * H], F32R)
        used = [0, 0]

        def place(parts, pattern, rounded=False, **dims):
            size = 1
            for d in dims.values():
                size *= d
            at = used[rounded]
            used[rounded] += size
            return (room_r if rounded else room)[0:parts, at:at + size].rearrange(pattern, **dims)

        ctx_sb = place(TP, "p (j c d) -> p j c d", j=PARTS, c=CPP, d=H)
        v_sb = place(TP, "p (b h x) -> p b h x", b=4, h=NH, x=SW)
        v_pair = v_sb.rearrange("p (n c) h x -> p n c h x", c=2)
        p_sb = place(TP, "p (b k q) -> p b k q", b=3, k=KH, q=HPH * S)
        gate_sb = sb("gate_sb", [128, KH, E])
        sg_sb = sb("sg_sb", [128, KH, F])
        su_sb = sb("su_sb", [128, KH, F])
        sd_sb = sb("sd_sb", [F, H])
        wgu_sb = sb("wgu_sb", [128, QUAD, GE, 2, KH, F])
        wd_sb = sb("wd_sb", [F, QUAD, GE, H])
        wT = sb("wT", [128, 2, KH, H])
        wkv_hi = sb("wkv_hi", [128, 2, KH, H], F32R)
        wkv_lo = sb("wkv_lo", [128, 2, KH, H], F32R)
        attend = sb("attend", [TP, B, CH])
        sc_scale = sb("sc_scale", [TP, B, CH])
        sc_bias = sb("sc_bias", [TP, B, CH])
        stats = sb("stats", [TT, NT, 6])
        mv = sb("mv", [TT, NT, 2])
        std = sb("std", [TT, NT])
        rstd = sb("rstd", [TT, NT])
        xn = sb("xn", [TT, NT, H])
        xh = sb("xh", [TT, NT, H])
        clean_a = sb("clean_a", [128, NT * H])
        clean_m = sb("clean_m", [128, NT * H], I32)
        xT = sb("xT", [128, KH, TOK])
        q_raw = sb("q_raw", [128, KH, TOK])
        qT = sb("qT", [128, KH, TOK])
        q_hi = sb("q_hi", [128, KH, TOK], F32R)
        q_lo = sb("q_lo", [128, KH, TOK], F32R)
        q_bd = place(128, "p (b l k h s) -> p b l k h s", True, b=2, l=2, k=KH, h=HPH, s=S)
        cT_hi = place(128, "p (b k c t) -> p b k c t", True, b=2, k=KH, c=2, t=TPE)
        cT_lo = place(128, "p (b k c t) -> p b k c t", True, b=2, k=KH, c=2, t=TPE)
        kT_hi = place(128, "p (b j t) -> p b j t", True, b=2, j=KH, t=2 * TPE)
        kT_lo = place(128, "p (b j t) -> p b j t", True, b=2, j=KH, t=2 * TPE)
        kT = sb("kT", [128, KH, 2 * TPE])
        o_all = sb("o_all", [128, NT, B, S])
        den = sb("den", [TT, NT * NH])
        rden = sb("rden", [TT, NT * NH])
        psum_p = sb("psum_p", [TT, NT * NH])
        ao = sb("ao", [TT, NT, H])
        delta = sb("delta", [TT, NT, H])
        x1 = sb("x1", [TT, NT, H])
        neg = sb("neg", [TT, NT, E])
        score = sb("score", [TT, NT, E])
        biased = sb("biased", [TT, NT, E])
        top_g = sb("top_g", [TT, NT, NG, 8])
        gsc = sb("gsc", [TT, NT, NG + 8])
        top8 = sb("top8", [TT, NT, 8])
        g_left = sb("g_left", [TT, NT, NG + 8])
        g_pick = sb("g_pick", [TT, NT, NG])
        g_off = sb("g_off", [TT, NT, NG])
        cand = sb("cand", [TT, NT, E + 8])
        e_left = sb("e_left", [TT, NT, E + 8])
        pick = sb("pick", [TT, NT, E])
        wsum = sb("wsum", [TT, NT])
        wtok = sb("wtok", [TT, NT, E])
        fits = sb("fits", [TT, NT, E])
        slot = sb("slot", [TT, NT, E])
        used = [0, 0]
        xn_hi = place(TT, "p (i d) -> p i d", True, i=NT, d=H)
        xn_lo = place(TT, "p (i d) -> p i d", True, i=NT, d=H)
        put = place(TT, "p (b i e s) -> p b i e s", True, b=2, i=NT, e=GE, s=SLOT)
        putT = place(128, "p (b c t) -> p b c t", True, b=2, c=2, t=TOK)
        eo_hi = place(128, "p (b c d) -> p b c d", True, b=2, c=2, d=H)
        eo_lo = place(128, "p (b c d) -> p b c d", True, b=2, c=2, d=H)
        put_b = place(TT, "p (b x) -> p b x", b=2, x=NT * GE * SLOT // 2).bitcast(BF16).rearrange(
            "p b (i x) -> p b i x", i=NT)
        act_g = place(128, "p (b c f) -> p b c f", b=2, c=2, f=F)
        h_sb = place(128, "p (b c f) -> p b c f", b=2, c=2, f=F)
        hT = place(F, "p (b x) -> p b x", b=2, x=GE * SLOT)
        bufT = sb("bufT", [128, 2, KH, GE, SLOT])
        w3 = place(TT, "p (i x) -> p i x", i=NT, x=E * 3 // 2).bitcast(BF16).rearrange("p i (e w) -> p i e w", w=3)
        w_rest = neg
        slot_w = sb("slot_w", [128, 2, 2])
        sh_g, sh_h = q_raw[0:F, 0, :], qT[0:F, 0, :]
        y_sb = xh

        x_in, w_in, b_in, mask_in_s, small_in = sem("x_in"), sem("w_in"), sem("b_in"), sem("mask_in"), sem("small_in")
        ctx_loaded = [sem(f"ctx_loaded{j}") for j in range(PARTS)]
        ew_loaded = [sem(f"ew_loaded{j}") for j in range(QUAD)]
        out_done = sem("out_done")
        pool_step, consts, dve_step = sem("pool_step"), sem("consts"), sem("dve_step")
        var_ready, std_ready = sem("var_ready"), sem("std_ready")
        wT_psum, wT_ready, w_lo_ready = sem("wT_psum"), sem("wT_ready"), sem("w_lo_ready")
        xh_ready, xT_psum, xT_ready = sem("xh_ready"), sem("xT_psum"), sem("xT_ready")
        q_psum, qT_ready, qbd_ready, mask_ready = sem("q_psum"), sem("qT_ready"), sem("qbd_ready"), sem("mask_ready")
        cT_psum, cT_hi_ready, cT_ready = sem("cT_psum"), sem("cT_hi_ready"), sem("cT_ready")
        k_psum, kv_psum, k_raw, k_hi_ready, kT_ready, v_ready = (sem("k_psum"), sem("kv_psum"), sem("k_raw"), sem("k_hi_ready"),
                                                         sem("kT_ready"), sem("v_ready"))
        s_psum, exp_done, p_ready, pv_done, o_saved = (sem("s_psum"), sem("exp_done"), sem("p_ready"),
                                                       sem("pv_done"), sem("o_saved"))
        oT_psum, ao_ready, aoT_psum, aoT_ready, od_psum = (sem("oT_psum"), sem("ao_ready"), sem("aoT_psum"),
                                                           sem("aoT_ready"), sem("od_psum"))
        logit_psum, neg_ready = sem("logit_psum"), sem("neg_ready")
        sh_psum, shg_ready, shh_ready = sem("sh_psum"), sem("shg_ready"), sem("shh_ready")
        pick_ready, pos_psum = sem("pick_ready"), sem("pos_psum")
        xs_ready = sem("xs_ready")
        put_ready, putb_ready = sem("put_ready"), sem("putb_ready")
        buf_psum, buf_ready = sem("buf_psum"), sem("buf_ready")
        gu_psum, actg_ready, sw_ready, h_ready = sem("gu_psum"), sem("actg_ready"), sem("sw_ready"), sem("h_ready")
        hT_psum, hT_ready = sem("hT_psum"), sem("hT_ready")
        z_psum, z_saved, eo_ready = sem("z_psum"), sem("z_saved"), sem("eo_ready")
        combined = sem("combined")
        y_ready = sem("y_ready")

        block = st.enter_context(nc.Block())

        turned_bank = PS[:, 0, 0:KH * 2 * TP].rearrange("p (k c t) -> p k c t", k=KH, c=2)
        key_bank = PS[:, 1, 0:KH * 2 * TPE].rearrange("p (j t) -> p j t", j=KH)
        value_bank = PS[0:TP, 2, :].rearrange("p (c d) -> p c d", c=2)

        def score_banks(n):
            return PS[0:TP, 3 + 2 * (n % 2):5 + 2 * (n % 2), 0:HPH * S]

        def y_bank(i):
            return PS[0:TT, i // 2, (i % 2) * H:(i % 2 + 1) * H]

        def buf_bank(g):
            return PS[:, 2 + g % 2, 0:KH * GE * CAP].rearrange("p (k s) -> p k s", k=KH)

        gu_bank = PS[:, 4, 0:4 * F].rearrange("p (c u f) -> p c u f", c=2, u=2)
        sw_bank = PS[:, 4, 4 * F:4 * F + 12].rearrange("p (c e w) -> p c e w", c=2, e=2)
        hT_bank = PS[0:F, 5, 0:GE * SLOT]

        def after(eng, s, value):
            if isinstance(value, int) and value <= 0:
                return
            eng.wait_ge(s, value)

        ctx_v = ctx_in.rearrange("b (p c) d -> b p c d", c=CH)
        x_v = x.rearrange("b s d -> (b s) d").rearrange("(i p) d -> p i d", p=TT)
        out_v = out.rearrange("b s d -> (b s) d").rearrange("(i p) d -> p i d", p=TT)
        wg_v = w_gate.rearrange("e (p k) f -> p e k f", k=KH)
        wu_v = w_up.rearrange("e (p k) f -> p e k f", k=KH)
        wd_v = w_down.rearrange("e f d -> f e d")

        @block.sync
        def _(sp):
            def load_ctx(b, j):
                sp.dma_start(ctx_sb[:, j], ctx_v[b, :, j * CPP:(j + 1) * CPP, :]).then_inc(ctx_loaded[j], 16)

            def load_experts(g, c):
                for u, w in enumerate((wg_v, wu_v)):
                    sp.dma_start(wgu_sb[:, c, :, u], w[:, bass.ds(g * GE, GE)]).then_inc(ew_loaded[c], 16)
                sp.dma_start(wd_sb[:, c], wd_v[:, bass.ds(g * GE, GE)]).then_inc(ew_loaded[c], 16)

            sp.dma_start(x_sb[:], x_v).then_inc(x_in, 16)
            load_ctx(0, 0)
            for w, src in enumerate((Wq, Wk, Wv, Wo)):
                sp.dma_start(w_raw[:, w], src.rearrange("(o p) k -> p o k", p=128)).then_inc(w_in, 16)
            load_ctx(0, 1)
            load_ctx(0, 2)
            for c in range(QUAD):
                load_experts(c, c)

            with sp.Fori(1, B) as b:
                for j in range(PARTS):
                    sp.wait_ge(cT_psum, b * PAIRS - PAIRS + (j + 1) * CPP // 2)
                    load_ctx(b, j)
            with sp.Fori(1, GROUPS // QUAD) as q:
                for c in range(QUAD):
                    sp.wait_ge(z_psum, (q * QUAD - QUAD + c + 1) * 3)
                    load_experts(q * QUAD + c, c)
            for i in range(2):
                sp.wait_ge(y_ready, i + 1)
                sp.dma_start(out_v[:, 2 * i:2 * i + 2], y_sb[:, 2 * i:2 * i + 2]).then_inc(out_done, 16)
            sp.wait_ge(out_done, 32)

        @block.gpsimd
        def _(pool):
            done = [0]

            def step(ins):
                done[0] += 1
                ins.then_inc(pool_step, 1)
                pool.wait_ge(pool_step, done[0])

            step(nc.gpsimd.memset(ident[:], 0.0))
            step(nc.gpsimd.affine_select(out=ident[:], in_=ident[:], compare_op=ALU.not_equal, fill=1.0, base=0,
                                         pattern=[[-1, 128]], channel_multiplier=1))
            step(nc.gpsimd.tensor_copy(ident_b[:], ident[:]))
            step(nc.gpsimd.memset(head_mask[:], 1.0))
            step(nc.gpsimd.affine_select(out=head_mask[:], in_=head_mask[:], compare_op=ALU.is_ge, fill=0.0, base=0,
                                         pattern=[[-HD, HPH]], channel_multiplier=1))
            step(nc.gpsimd.affine_select(out=head_mask[:], in_=head_mask[:], compare_op=ALU.is_ge, fill=0.0,
                                         base=HD - 1, pattern=[[HD, HPH]], channel_multiplier=-1))
            step(nc.gpsimd.memset(v_sb, 1.0))
            step(nc.gpsimd.memset(cT_hi.bitcast(F32), 0.0))
            step(nc.gpsimd.memset(cT_lo.bitcast(F32), 0.0))
            step(nc.gpsimd.memset(bufT[:], 0.0))
            step(nc.gpsimd.memset(ones[:], 1.0))
            step(nc.gpsimd.memset(before[:], 1.0))
            step(nc.gpsimd.affine_select(out=before[:], in_=before[:], compare_op=ALU.is_ge, fill=0.0, base=-1,
                                         pattern=[[1, TT]], channel_multiplier=-1))
            nc.gpsimd.iota(slot_no[:], pattern=[[1, SLOT]], base=0, channel_multiplier=0,
                           allow_small_or_imprecise_dtypes=True).then_inc(consts, 1)

            def place_queries(b):
                for half, q in enumerate((q_hi, q_lo)):
                    nc.gpsimd.tensor_tensor(
                        q_bd[:, b % 2, half],
                        q[:, :, bass.ds(b * S, S)].bitcast(F32).unsqueeze(2).to_broadcast([128, KH, HPH, S]),
                        head_mask[:].unsqueeze(1).unsqueeze(3).to_broadcast([128, KH, HPH, S]),
                        ALU.mult).then_inc(qbd_ready, 1)

            pool.wait_ge(qT_ready, 1)
            place_queries(0)
            place_queries(1)
            with pool.Fori(2, B) as b:
                pool.wait_ge(s_psum, b * CH - CH)
                place_queries(b)

            def narrow(g, c):
                pool.wait_ge(put_ready, g + 1)
                after(pool, z_psum, (g - 2) * 3 + 2)
                after(pool, gu_psum, g - 1)
                p = put[:, c % 2].bitcast(F32).rearrange("p i e s -> p i (e s)")
                nc.gpsimd.tensor_tensor(put_b[:, c % 2], p, p, ALU.mult).then_inc(putb_ready, 1)

            for c in range(QUAD):
                narrow(c, c)
            with pool.Fori(1, GROUPS // QUAD) as q:
                for c in range(QUAD):
                    narrow(q * QUAD + c, c)

        @block.scalar
        def _(act):
            act.dma_start(bqk[:, 0], bq.rearrange("(j p) -> p j", p=128), allow_slow_non_contiguous=True).then_inc(b_in, 16)
            act.dma_start(bqk[:, 1], bk.rearrange("(j p) -> p j", p=128), allow_slow_non_contiguous=True).then_inc(b_in, 16)
            act.dma_start(bv_bc[:], bv.partition_broadcast(128)).then_inc(b_in, 16)
            act.dma_start(mask_i[:], mask_in.rearrange("b (p c) -> p b c", c=CH)).then_inc(mask_in_s, 16)
            small = ((bo_bc, bo), (gamma_bc, gamma), (beta_bc, beta), (rbias_bc, rbias), (rs_bc, rs))
            for dst, src in small:
                act.dma_start(dst[:], src.partition_broadcast(TT)).then_inc(small_in, 16)
            act.dma_start(gate_sb[:], gate_w.rearrange("(k p) e -> p k e", p=128)).then_inc(small_in, 16)
            act.dma_start(sg_sb[:], ws_gate.rearrange("(k p) e -> p k e", p=128)).then_inc(small_in, 16)
            act.dma_start(su_sb[:], ws_up.rearrange("(k p) e -> p k e", p=128)).then_inc(small_in, 16)
            act.dma_start(sd_sb[:], ws_down).then_inc(small_in, 16)

            def root(n):
                act.wait_ge(var_ready, n)
                nc.scalar.activation(std[:], std[:], ACT.Sqrt).then_inc(std_ready, 1)

            root(1)
            for w, dst in enumerate((wT[:, 0], wkv_hi[:, 0], wkv_hi[:, 1], wT[:, 1])):
                act.wait_ge(wT_psum, w + 1)
                nc.scalar.copy(dst, PS[:, w, :].rearrange("p (k o) -> p k o", k=KH)).then_inc(wT_ready, 1)

            def context_hi(n, m):
                act.wait_ge(cT_psum, n + 1)
                after(act, kv_psum, n - 1)
                nc.scalar.copy(cT_hi[:, m % 2, :, :, 0:TP], turned_bank).then_inc(cT_hi_ready, 1)

            def keys_hi(n, m):
                act.wait_ge(k_raw, n + 1)
                after(act, s_psum, n * 2 - 2)
                nc.scalar.copy(kT_hi[:, m % 2], kT[:]).then_inc(k_hi_ready, 1)

            def exps(n, b, c):
                act.wait_ge(s_psum, n + 1)
                after(act, pv_done, n - 2)
                nc.scalar.activation(p_sb[:, c % 3], score_banks(c), ACT.Exp, bias=sc_bias[:, b, c:c + 1],
                                     scale=sc_scale[:, b, c:c + 1]).then_inc(exp_done, 1)

            def batch(b, last):
                for m in range(PAIRS):
                    n = b * PAIRS + m
                    exps(n * 2, b, 2 * m)
                    if m + 1 < PAIRS or not last:
                        keys_hi(n + 1, m + 1)
                    exps(n * 2 + 1, b, 2 * m + 1)
                    if m + 2 < PAIRS or not last:
                        context_hi(n + 2, m + 2)

            context_hi(0, 0)
            context_hi(1, 1)
            keys_hi(0, 0)
            act.wait_ge(xT_psum, 1)
            nc.scalar.copy(xT[:], PS[:, 4:6, 0:TOK]).then_inc(xT_ready, 1)
            act.wait_ge(mask_ready, 1)
            batch(0, False)
            with act.Fori(1, B - 1) as b:
                batch(b, False)
            batch(B - 1, True)

            act.wait_ge(aoT_psum, 1)
            nc.scalar.copy(xT[:], PS[:, 4:6, 0:TOK]).then_inc(aoT_ready, 1)
            root(2)
            root(3)
            act.wait_ge(xT_psum, 2)
            nc.scalar.copy(xT[:], PS[:, 4:6, 0:TOK]).then_inc(xT_ready, 1)
            act.wait_ge(logit_psum, 1)
            nc.scalar.activation(neg[:], PS[0:TT, 6, 0:NT * E].rearrange("p (i e) -> p i e", i=NT), ACT.Exp,
                                 scale=-1.0).then_inc(neg_ready, 1)
            act.wait_ge(sh_psum, 1)
            nc.scalar.activation(sh_g, PS[0:F, 2, 0:TOK], ACT.Silu).then_inc(shg_ready, 1)

            def group(g, c):
                act.wait_ge(gu_psum, g + 1)
                after(act, h_ready, (g - 1) * 2)
                nc.scalar.activation(act_g[:, c % 2], gu_bank[:, :, 0, :], ACT.Silu).then_inc(actg_ready, 1)
                after(act, combined, g - 1)
                for p in range(2):
                    act.wait_ge(z_psum, g * 3 + p + 1)
                    nc.scalar.copy(putT[:, c % 2, p], PS[:, 6 + (3 * c + p) % 2, 0:TOK // 2].bitcast(BF16)
                                   ).then_inc(z_saved, 1)
                act.wait_ge(hT_psum, g + 1)
                after(act, z_psum, (g - 1) * 3)
                nc.scalar.copy(hT[:, c % 2], hT_bank).then_inc(hT_ready, 1)
                act.wait_ge(z_psum, g * 3 + 3)
                nc.scalar.copy(eo_hi[:, c % 2], PS[:, 6 + (3 * c + 2) % 2, :].rearrange("p (k d) -> p k d", k=2)
                               ).then_inc(z_saved, 1)

            for c in range(QUAD):
                group(c, c)
            with act.Fori(1, GROUPS // QUAD) as q:
                for c in range(QUAD):
                    group(q * QUAD + c, c)

        @block.vector
        def _(dve):
            done = [0]

            def step(ins):
                done[0] += 1
                ins.then_inc(dve_step, 1)
                dve.wait_ge(dve_step, done[0])

            def clean(dst, src, parts, cols):
                a, m = clean_a[0:parts, 0:cols], clean_m[0:parts, 0:cols]
                step(nc.vector.tensor_scalar(m, src, 0.0, 0.0, ALU.mult, ALU.is_equal))
                step(nc.vector.tensor_scalar(a, src, 0.0, LIMIT, ALU.max, ALU.min))
                step(nc.vector.tensor_scalar(dst, src, 0.0, -LIMIT, ALU.min, ALU.max))
                step(nc.vector.tensor_tensor(dst, dst, a, ALU.add))
                step(nc.vector.copy_predicated(dst, m, src))

            def layernorm(n, dst, src):
                for i in range(NT):
                    step(nc.vector.bn_stats(stats[:, i], src[:, i]))
                for i in range(NT):
                    step(nc.vector.bn_aggr(mv[:, i], stats[:, i]))
                nc.vector.tensor_scalar(std[:], mv[:, :, 1], EPS, None, ALU.add).then_inc(var_ready, 1)
                dve.wait_ge(std_ready, n)
                step(nc.vector.reciprocal(rstd[:], std[:]))
                for i in range(NT):
                    step(nc.vector.tensor_scalar(dst[:, i], src[:, i], mv[:, i, 0:1], rstd[:, i:i + 1],
                                                 ALU.subtract, ALU.mult))

            def flat(t):
                return t.rearrange("p i d -> p (i d)")

            dve.wait_ge(x_in, 16)
            layernorm(1, xn, x_sb)
            clean(flat(xh[:]), flat(xn[:]), TT, NT * H)
            nc.vector.memset(gsc[:, :, NG:], TOP_SENTINEL).then_inc(xh_ready, 1)
            step(nc.vector.memset(cand[:, :, E:], TOP_SENTINEL))
            dve.wait_ge(mask_in_s, 16)
            step(nc.vector.tensor_copy(attend[:], mask_i[:]))
            step(nc.vector.tensor_scalar(attend[:], attend[:], 0.5, None, ALU.is_gt))
            step(nc.vector.tensor_scalar(sc_scale[:], attend[:], 1.0 / HD ** 0.5, None, ALU.mult))
            nc.vector.tensor_scalar(sc_bias[:], attend[:], 50.0, -50.0, ALU.mult, ALU.add).then_inc(mask_ready, 1)
            for w in range(2):
                dve.wait_ge(wT_ready, w + 2)
                nc.vector.tensor_tensor(wkv_lo[:, w], PS[:, 1 + w, :].rearrange("p (k o) -> p k o", k=KH),
                                        wkv_hi[:, w].bitcast(F32), ALU.subtract).then_inc(w_lo_ready, 1)
            dve.wait_ge(b_in, 48)

            def context_lo(n, m):
                dve.wait_ge(cT_hi_ready, n + 1)
                after(dve, kv_psum, n - 1)
                nc.vector.tensor_tensor(cT_lo[:, m % 2, :, :, 0:TP], turned_bank,
                                        cT_hi[:, m % 2, :, :, 0:TP].bitcast(F32), ALU.subtract).then_inc(cT_ready, 1)

            def keys(n, m):
                dve.wait_ge(k_psum, n + 1)
                after(dve, kT_ready, n)
                nc.vector.tensor_tensor(kT[:], key_bank, bqk[:, 1].unsqueeze(2).to_broadcast([128, KH, 2 * TPE]),
                                        ALU.add).then_inc(k_raw, 1)

            def keys_lo(n, m):
                dve.wait_ge(k_hi_ready, n + 1)
                after(dve, s_psum, n * 2 - 2)
                nc.vector.tensor_tensor(kT_lo[:, m % 2], kT[:], kT_hi[:, m % 2].bitcast(F32),
                                        ALU.subtract).then_inc(kT_ready, 1)

            def values(n, m):
                dve.wait_ge(kv_psum, n + 1)
                after(dve, pv_done, n * 2 - 2)
                nc.vector.tensor_tensor(
                    v_pair[:, m % 2, :, :, 0:HD], value_bank.rearrange("p c (h d) -> p (c h) d", d=HD).rearrange("p (c h) d -> p c h d", c=2),
                    bv_bc[0:TP].rearrange("p (h d) -> p h d", h=NH).unsqueeze(1).to_broadcast([TP, 2, NH, HD]),
                    ALU.add).then_inc(v_ready, 1)

            def clip(n, c):
                dve.wait_ge(exp_done, n + 1)
                nc.vector.tensor_scalar(p_sb[:, c % 3], p_sb[:, c % 3], EXP_MIN, EXP_MAX, ALU.max, ALU.min).then_inc(p_ready, 1)

            def batch(b, last):
                for m in range(PAIRS):
                    n = b * PAIRS + m
                    more = m + 1 < PAIRS or not last
                    clip(n * 2, 2 * m)
                    if more:
                        keys(n + 1, m + 1)
                        keys_lo(n + 1, m + 1)
                    clip(n * 2 + 1, 2 * m + 1)
                    if m + 2 < PAIRS or not last:
                        context_lo(n + 2, m + 2)
                    if more:
                        values(n + 1, m + 1)
                dve.wait_ge(pv_done, b * CH + CH)
                nc.vector.tensor_copy(o_all[:, :, b, :], PS[:, 7, 0:NT * S].rearrange("p (g s) -> p g s", g=NT)).then_inc(o_saved, 1)

            dve.wait_ge(consts, 1)
            context_lo(0, 0)
            context_lo(1, 1)
            keys(0, 0)
            keys_lo(0, 0)
            values(0, 0)
            dve.wait_ge(q_psum, 1)
            for j in range(KH):
                step(nc.vector.tensor_scalar(q_raw[:, j], PS[:, 6 + j, 0:TOK], bqk[:, 0, j:j + 1], None, ALU.add))
            clean(flat(qT[:]), flat(q_raw[:]), 128, KH * TOK)
            step(nc.vector.tensor_copy(q_hi[:], qT[:]))
            nc.vector.tensor_tensor(q_lo[:], qT[:], q_hi[:].bitcast(F32), ALU.subtract).then_inc(qT_ready, 1)
            batch(0, False)
            with dve.Fori(1, B - 1) as b:
                batch(b, False)
            batch(B - 1, True)

            dve.wait_ge(oT_psum, 1)
            heads = PS[0:TT, 0:4, :].rearrange("p b (h x) -> p (b h) x", x=SW)
            step(nc.vector.tensor_copy(den[:], heads[:, :, HD]))
            step(nc.vector.reciprocal(rden[:], den[:]))
            step(nc.vector.tensor_tensor(psum_p[:], den[:], rden[:], ALU.mult))
            step(nc.vector.tensor_scalar(psum_p[:], psum_p[:], 1e-8, None, ALU.add))
            step(nc.vector.reciprocal(psum_p[:], psum_p[:]))
            step(nc.vector.tensor_tensor(rden[:], rden[:], psum_p[:], ALU.mult))
            nc.vector.tensor_tensor(ao[:].rearrange("p i (h d) -> p (i h) d", d=HD), heads[:, :, 0:HD],
                                    rden[:].unsqueeze(2).to_broadcast([TT, NT * NH, HD]), ALU.mult).then_inc(ao_ready, 1)
            dve.wait_ge(small_in, 9 * 16)
            step(nc.vector.tensor_scalar(rs_bc[:], rs_bc[:], 0.0, 0.3, ALU.max, ALU.min))
            dve.wait_ge(od_psum, 1)
            for i in range(2):
                step(nc.vector.tensor_tensor(xn[:, 2 * i:2 * i + 2], PS[0:TT, 6 + i, :].rearrange("p (i d) -> p i d", i=2),
                                             bo_bc[:].unsqueeze(1).to_broadcast([TT, 2, H]), ALU.add))
            clean(flat(delta[:]), flat(xn[:]), TT, NT * H)
            step(nc.vector.tensor_scalar(flat(delta[:]), flat(delta[:]), rs_bc[:, 0:1], None, ALU.mult))
            layernorm(2, xn, delta)
            step(nc.vector.tensor_tensor(xn[:], xn[:], gamma_bc[:].unsqueeze(1).to_broadcast([TT, NT, H]), ALU.mult))
            step(nc.vector.tensor_tensor(xn[:], xn[:], beta_bc[:].unsqueeze(1).to_broadcast([TT, NT, H]), ALU.add))
            step(nc.vector.tensor_tensor(x1[:], x_sb[:], xn[:], ALU.add))
            layernorm(3, xn, x1)
            nc.vector.memset(den[:], 0.0).then_inc(xh_ready, 1)

            dve.wait_ge(neg_ready, 1)
            step(nc.vector.tensor_scalar(neg[:], neg[:], 1.0, None, ALU.add))
            step(nc.vector.reciprocal(score[:], neg[:]))
            step(nc.vector.tensor_tensor(biased[:], score[:], rbias_bc[:].unsqueeze(1).to_broadcast([TT, NT, E]), ALU.add))
            for i in range(NT):
                for k in range(NG):
                    ins = nc.vector.max(top_g[:, i, k], biased[:, i, k * EPG:(k + 1) * EPG])
                step(ins)
            step(nc.vector.tensor_tensor(gsc[:, :, 0:NG], top_g[:, :, :, 0], top_g[:, :, :, 1], ALU.add))

            def first_best(values, best, left, width, count):
                for i in range(NT):
                    step(nc.vector.max(best[:, i], values[:, i, 0:width]))
                step(nc.vector.memset(best[:, :, count:8], TOP_SENTINEL))
                for i in range(NT):
                    step(nc.vector.match_replace(left[:, i], best[:, i], values[:, i], TAKEN))

            first_best(gsc, top8, g_left, NG, TOPG)
            step(nc.vector.tensor_scalar(g_pick[:], g_left[:, :, 0:NG], TAKEN, None, ALU.is_equal))
            step(nc.vector.tensor_scalar(g_off[:], g_pick[:], HUGE, -HUGE, ALU.mult, ALU.add))
            cand_g = cand[:, :, 0:E].rearrange("p i (k e) -> p i k e", k=NG)
            step(nc.vector.tensor_tensor(cand_g, biased[:].rearrange("p i (k e) -> p i k e", k=NG),
                                         g_pick[:].unsqueeze(3).to_broadcast([TT, NT, NG, EPG]), ALU.mult))
            step(nc.vector.tensor_tensor(cand_g, cand_g, g_off[:].unsqueeze(3).to_broadcast([TT, NT, NG, EPG]), ALU.add))
            first_best(cand, top8, e_left, E, TOPK)
            step(nc.vector.tensor_scalar(pick[:], e_left[:, :, 0:E], TAKEN, None, ALU.is_equal))
            nc.vector.tensor_tensor(wtok[:], score[:], pick[:], ALU.mult).then_inc(pick_ready, 1)
            dve.wait_ge(pick_ready, 1)
            step(nc.vector.tensor_reduce(wsum[:], wtok[:], AX.X, ALU.add))
            step(nc.vector.reciprocal(wsum[:], wsum[:]))
            step(nc.vector.tensor_tensor(wtok[:], wtok[:], wsum[:].unsqueeze(2).to_broadcast([TT, NT, E]), ALU.mult))
            step(nc.vector.tensor_scalar(wtok[:], wtok[:], SCALE, None, ALU.mult))
            rest = wtok
            for part in range(3):
                step(nc.vector.tensor_copy(w3[:, :, :, part], rest[:]))
                if part < 2:
                    step(nc.vector.tensor_tensor(w_rest[:], rest[:], w3[:, :, :, part], ALU.subtract))
                    rest = w_rest
            dve.wait_ge(pos_psum, 1)
            pos = PS[0:TT, 7, 0:NT * E].rearrange("p (i e) -> p i e", i=NT)
            step(nc.vector.tensor_scalar(fits[:], pos, float(CAP), None, ALU.is_lt))
            step(nc.vector.tensor_tensor(fits[:], fits[:], pick[:], ALU.mult))
            step(nc.vector.tensor_scalar(slot[:], pos, 1.0, None, ALU.add))
            step(nc.vector.tensor_tensor(slot[:], slot[:], fits[:], ALU.mult))
            step(nc.vector.tensor_scalar(slot[:], slot[:], -1.0, None, ALU.add))
            dve.wait_ge(shg_ready, 1)
            nc.vector.tensor_tensor(sh_h, sh_g, PS[0:F, 3, 0:TOK], ALU.mult).then_inc(shh_ready, 1)

            def routes(g, c):
                after(dve, buf_psum, g - 1)
                after(dve, putb_ready, g - 1)
                nc.vector.tensor_tensor(
                    put[:, c % 2], slot_no[:].unsqueeze(1).unsqueeze(1).to_broadcast([TT, NT, GE, SLOT]),
                    slot[:, :, bass.ds(g * GE, GE)].unsqueeze(3).to_broadcast([TT, NT, GE, SLOT]),
                    ALU.is_equal).then_inc(put_ready, 1)

            def gathered(g, c):
                dve.wait_ge(buf_psum, g + 1)
                after(dve, gu_psum, g - 1)
                nc.vector.tensor_copy(bufT[:, c % 2, :, :, 0:CAP], buf_bank(c).rearrange("p k (e s) -> p k e s", e=GE)
                                      ).then_inc(buf_ready, 1)

            def hidden(g, c):
                dve.wait_ge(actg_ready, g + 1)
                for e in range(2):
                    r = slice(e * SLOT, (e + 1) * SLOT)
                    nc.vector.tensor_reduce(slot_w[r, c % 2], sw_bank[r, :, e, :], AX.X, ALU.add).then_inc(sw_ready, 1)
                dve.wait_ge(sw_ready, g * 2 + 2)
                after(dve, hT_psum, g - 1)
                for p in range(2):
                    nc.vector.scalar_tensor_tensor(out=h_sb[:, c % 2, p], in0=act_g[:, c % 2, p],
                                                   scalar=slot_w[:, c % 2, p:p + 1], in1=gu_bank[:, p, 1, :],
                                                   op0=ALU.mult, op1=ALU.mult).then_inc(h_ready, 1)

            def outputs_lo(g, c):
                dve.wait_ge(z_saved, g * 3 + 3)
                after(dve, combined, g - 1)
                nc.vector.tensor_tensor(eo_lo[:, c % 2], PS[:, 6 + (3 * c + 2) % 2, :].rearrange("p (k d) -> p k d", k=2),
                                        eo_hi[:, c % 2].bitcast(F32), ALU.subtract).then_inc(eo_ready, 1)

            def quad(q, last):
                for c in range(QUAD):
                    g = q * QUAD + c
                    more = c + 1 < QUAD or not last
                    if more:
                        routes(g + 1, c + 1)
                    hidden(g, c)
                    if more:
                        gathered(g + 1, c + 1)
                    outputs_lo(g, c)

            routes(0, 0)
            step(nc.vector.tensor_copy(xn_hi, xn[:]))
            nc.vector.tensor_tensor(xn_lo, xn[:], xn_hi.bitcast(F32), ALU.subtract).then_inc(xs_ready, 1)
            gathered(0, 0)
            quad(0, False)
            with dve.Fori(1, GROUPS // QUAD - 1) as q:
                quad(q, False)
            quad(GROUPS // QUAD - 1, True)

            dve.wait_ge(combined, GROUPS)
            for i in range(2):
                nc.vector.tensor_tensor(y_sb[:, 2 * i:2 * i + 2], PS[0:TT, i, :].rearrange("p (i d) -> p i d", i=2),
                                        x1[:, 2 * i:2 * i + 2], ALU.add).then_inc(y_ready, 1)

        @block.tensor
        def _(pe):
            mm, turn = nc.tensor.matmul, nc.tensor.transpose

            pe.wait_ge(consts, 1)
            for w in range(4):
                if w == 0:
                    pe.wait_ge(w_in, 64)
                for k in range(KH):
                    for o in range(KH):
                        ins = turn(PS[:, w, k * H + o * 128:k * H + o * 128 + 128], w_raw[:, w, o, k * 128:k * 128 + 128], ident[:])
                ins.then_inc(wT_psum, 1)

            def turn_tokens(src, s):
                for k in range(KH):
                    for i in range(NT):
                        ins = turn(PS[:, 4 + k, i * TT:(i + 1) * TT], src[:, i, k * 128:(k + 1) * 128], ident[0:TT, 0:TT])
                ins.then_inc(s, 1)

            def turned(n, m, b):
                after(pe, cT_ready, n)
                if m % (CPP // 2) == 0:
                    pe.wait_ge(ctx_loaded[2 * m // CPP], (b + 1) * 16)
                for c in range(2):
                    ch = 2 * m + c
                    for k in range(KH):
                        ins = turn(turned_bank[:, k, c, :], ctx_sb[:, ch // CPP, ch % CPP, k * 128:(k + 1) * 128],
                                   ident[0:TP, 0:TP])
                ins.then_inc(cT_psum, 1)

            def project_keys(n, m):
                pe.wait_ge(cT_ready, n + 1)
                after(pe, k_raw, n)
                hi, lo = (t[:, m % 2].rearrange("p k c t -> p k (c t)") for t in (cT_hi, cT_lo))
                for j in range(KH):
                    js = slice(j * 128, (j + 1) * 128)
                    terms = [(w[:, 0, k, js], c[:, k, :]) for k in range(KH)
                             for w, c in ((wkv_hi, hi), (wkv_hi, lo), (wkv_lo, hi))]
                    for t, (w, c) in enumerate(terms):
                        ins = mm(key_bank[:, j, :], w, c, start=(t == 0), stop=(t == len(terms) - 1))
                ins.then_inc(k_psum, 1)

            def project_values(n, m):
                after(pe, v_ready, n)
                for c in range(2):
                    hi, lo = cT_hi[:, m % 2, :, c, 0:TP], cT_lo[:, m % 2, :, c, 0:TP]
                    terms = [(x[:, k, :], w[:, 1, k, :]) for k in range(KH)
                             for x, w in ((hi, wkv_hi), (hi, wkv_lo), (lo, wkv_hi))]
                    for t, (x, w) in enumerate(terms):
                        ins = mm(value_bank[:, c, :], x, w, start=(t == 0), stop=(t == len(terms) - 1))
                ins.then_inc(kv_psum, 1)

            def scores(n, c, b):
                after(pe, exp_done, n - 1)
                for j in range(KH):
                    q = [q_bd[:, b % 2, half, j].rearrange("p h s -> p (h s)") for half in range(2)]
                    hi, lo = (t[:, (c // 2) % 2, j, (c % 2) * TPE:(c % 2) * TPE + TP] for t in (kT_hi, kT_lo))
                    mm(score_banks(c)[:, j, :], hi, q[0], start=True, stop=False)
                    mm(score_banks(c)[:, j, :], hi, q[1], start=False, stop=False)
                    ins = mm(score_banks(c)[:, j, :], lo, q[0], start=False, stop=True)
                ins.then_inc(s_psum, 1)

            def weigh_values(n, m):
                pe.wait_ge(p_ready, n + 1)
                for h in range(NH):
                    i, g = h % NT, h // NT
                    ins = mm(PS[32 * i:32 * i + SW, 7, g * S:(g + 1) * S], v_sb[:, m % 4, h, :],
                             p_sb[:, m % 3, h // HPH, (h % HPH) * S:(h % HPH + 1) * S],
                             start=(m == 0 and g == 0), stop=(m == CH - 1), skip_group_check=True)
                ins.then_inc(pv_done, 1)

            def batch(b, last):
                pe.wait_ge(qbd_ready, b * 2 + 2)
                for m in range(PAIRS):
                    n = b * PAIRS + m
                    more = m + 1 < PAIRS or not last
                    pe.wait_ge(kT_ready, n + 1)
                    scores(n * 2, 2 * m, b)
                    if more:
                        project_keys(n + 1, m + 1)
                    if m == 1:
                        after(pe, o_saved, b)
                    if m > 0:
                        weigh_values(n * 2 - 2, 2 * m - 2)
                    scores(n * 2 + 1, 2 * m + 1, b)
                    if m > 0:
                        weigh_values(n * 2 - 1, 2 * m - 1)
                    if m + 2 < PAIRS or not last:
                        turned(n + 2, (m + 2) % PAIRS, b + (m + 2) // PAIRS)
                    if more:
                        project_values(n + 1, m + 1)
                for c in range(CH - 2, CH):
                    weigh_values(b * CH + c, c)

            pe.wait_ge(wT_ready, 4)
            turned(0, 0, 0)
            turned(1, 1, 0)
            pe.wait_ge(w_lo_ready, 2)
            project_keys(0, 0)
            project_values(0, 0)
            pe.wait_ge(xh_ready, 1)
            turn_tokens(xh, xT_psum)
            pe.wait_ge(xT_ready, 1)
            pe.wait_ge(wT_ready, 4)
            for j in range(KH):
                for k in range(KH):
                    ins = mm(PS[:, 6 + j, 0:TOK], wT[:, 0, k, j * 128:(j + 1) * 128], xT[:, k, :], start=(k == 0), stop=(k == KH - 1))
            ins.then_inc(q_psum, 1)

            batch(0, False)
            with pe.Fori(1, B - 1) as b:
                batch(b, False)
            batch(B - 1, True)

            pe.wait_ge(o_saved, B)
            for i in range(NT):
                for g in range(NT):
                    ins = turn(PS[0:TT, i, g * 128:(g + 1) * 128], o_all[:, g, 2 * i:2 * i + 2, :].rearrange("p b s -> p (b s)"), ident[:])
            ins.then_inc(oT_psum, 1)
            pe.wait_ge(ao_ready, 1)
            turn_tokens(ao, aoT_psum)
            pe.wait_ge(aoT_ready, 1)
            for i in range(NT):
                for k in range(KH):
                    ins = mm(PS[0:TT, 6 + i // 2, (i % 2) * H:(i % 2 + 1) * H], xT[:, k, i * TT:(i + 1) * TT], wT[:, 1, k, :],
                             start=(k == 0), stop=(k == KH - 1))
            ins.then_inc(od_psum, 1)

            pe.wait_ge(xh_ready, 2)
            turn_tokens(xn, xT_psum)
            pe.wait_ge(xT_ready, 2)
            for i in range(NT):
                for k in range(KH):
                    ins = mm(PS[0:TT, 6, i * E:(i + 1) * E], xT[:, k, i * TT:(i + 1) * TT], gate_sb[:, k, :],
                             start=(k == 0), stop=(k == KH - 1))
            ins.then_inc(logit_psum, 1)
            for u, w in enumerate((sg_sb, su_sb)):
                for k in range(KH):
                    ins = mm(PS[0:F, 2 + u, 0:TOK], w[:, k, :], xT[:, k, :], start=(k == 0), stop=(k == KH - 1))
            ins.then_inc(sh_psum, 1)
            pe.wait_ge(pick_ready, 1)
            for i in range(NT):
                for j in range(i + 1):
                    ins = mm(PS[0:TT, 7, i * E:(i + 1) * E], before[:] if j == i else ones[:], pick[:, j, :],
                             start=(j == 0), stop=(j == i))
            ins.then_inc(pos_psum, 1)
            pe.wait_ge(shh_ready, 1)
            for i in range(NT):
                mm(y_bank(i), sh_h[:, i * TT:(i + 1) * TT], sd_sb[:], start=(i % 2 == 0), stop=False, skip_group_check=True)

            def gather(g, c):
                pe.wait_ge(put_ready, g + 1)
                after(pe, buf_ready, g - 1)
                for k in range(KH):
                    for i in range(NT):
                        for part in (xn_hi, xn_lo):
                            ins = mm(buf_bank(c)[:, k, :], part[:, i, k:H:KH], put[:, c % 2, i, :, 0:CAP],
                                     start=(i == 0 and part is xn_hi), stop=(i == NT - 1 and part is xn_lo))
                ins.then_inc(buf_psum, 1)

            def gate_up(g, c, q):
                pe.wait_ge(buf_ready, g + 1)
                pe.wait_ge(ew_loaded[c], (q + 1) * 48)
                after(pe, h_ready, g * 2)
                for p in range(2):
                    for k in range(KH):
                        for e in range(2):
                            mm(gu_bank[e * SLOT:(e + 1) * SLOT, p], bufT[:, c % 2, k, 2 * p + e, :],
                               wgu_sb[:, c, 2 * p + e, :, k, :], start=(k == 0), stop=(k == KH - 1), skip_group_check=True)
                pe.wait_ge(putb_ready, g + 1)
                for p in range(2):
                    for i in range(NT):
                        ins = mm(sw_bank[:, p].rearrange("p e w -> p (e w)"), put_b[:, c % 2, i, 2 * p * SLOT:2 * (p + 1) * SLOT],
                                 w3[:, i, bass.ds(g * GE + 2 * p, 2), :].rearrange("p e w -> p (e w)"),
                                 start=(i == 0), stop=(i == NT - 1), skip_group_check=True)
                ins.then_inc(gu_psum, 1)

            def turn_put(g, c):
                for p in range(2):
                    if p == 0:
                        after(pe, z_saved, g * 3 - 1)
                    else:
                        after(pe, eo_ready, g)
                    for i in range(NT):
                        ins = turn(PS[:, 6 + (3 * c + p) % 2, :].bitcast(BF16)[:, i * TT:(i + 1) * TT],
                                   put_b[:, c % 2, i, 2 * p * SLOT:2 * (p + 1) * SLOT], ident_b[0:TT, 0:TT])
                    ins.then_inc(z_psum, 1)

            def turn_hidden(g, c):
                pe.wait_ge(h_ready, g * 2 + 2)
                after(pe, hT_ready, g)
                for p in range(2):
                    ins = turn(hT_bank[:, p * 128:(p + 1) * 128], h_sb[:, c % 2, p], ident[:])
                ins.then_inc(hT_psum, 1)

            def down(g, c):
                pe.wait_ge(hT_ready, g + 1)
                pe.wait_ge(z_saved, g * 3 + 1)
                for e in range(GE):
                    r = SLOT * (e % 2)
                    ins = mm(PS[r:r + SLOT, 6 + (3 * c + 2) % 2, (e // 2) * H:(e // 2 + 1) * H],
                             hT[:, c % 2, e * SLOT:(e + 1) * SLOT], wd_sb[:, c, e, :],
                             start=True, stop=True, skip_group_check=True)
                ins.then_inc(z_psum, 1)

            def combine(g, c):
                pe.wait_ge(eo_ready, g + 1)
                for p in range(2):
                    for i in range(NT):
                        for part in (eo_hi, eo_lo):
                            ins = mm(y_bank(i), putT[:, c % 2, p, i * TT:(i + 1) * TT], part[:, c % 2, p, :],
                                     start=False, stop=True, skip_group_check=True)
                ins.then_inc(combined, 1)

            def quad(q, first, last):
                for c in range(QUAD):
                    g = q * QUAD + c
                    gate_up(g, c, q)
                    turn_put(g, c)
                    if c + 1 < QUAD or not last:
                        gather(g + 1, c + 1)
                    turn_hidden(g, c)
                    if c > 0 or not first:
                        combine(g - 1, c + 1)
                    down(g, c)

            pe.wait_ge(xs_ready, 1)
            gather(0, 0)
            quad(0, True, False)
            with pe.Fori(1, GROUPS // QUAD - 1) as q:
                quad(q, False, False)
            quad(GROUPS // QUAD - 1, False, True)
            combine(GROUPS - 1, QUAD - 1)


_INS = ["x", "ctx_2048", "mask_BxS2_ik0", "L0_xattn_Wq", "L0_xattn_bq", "L0_xattn_Wk", "L0_xattn_bk", "L0_xattn_Wv",
        "L0_xattn_bv", "L0_xattn_Wo", "L0_xattn_bo", "L0_xattn_ln_gamma", "L0_xattn_ln_beta",
        "L0_xattn_residual_scale", "L0_ffn_gate_w", "L0_ffn_bias", "L0_ffn_w_gate", "L0_ffn_w_up", "L0_ffn_w_down",
        "L0_ffn_ws_gate", "L0_ffn_ws_up", "L0_ffn_ws_down"]


def kernel(**inputs):
    import numpy as np
    import concourse.bacc as bacc
    from concourse.bass_utils import run_bass_kernel_spmd

    nc = bacc.Bacc("TRN2", target_bir_lowering=False, num_devices=1)
    arrays, args = {}, []
    for name in _INS:
        a = np.ascontiguousarray(inputs[name])
        if a.ndim == 0:
            a = a.reshape(1)
        arrays[f"in_{name}"] = a
        args.append(nc.dram_tensor(f"in_{name}", a.shape, mybir.dt.from_np(a.dtype), kind="ExternalInput").ap())
    args.append(nc.dram_tensor("out_0", (B, S, H), F32, kind="ExternalOutput").ap())
    build(nc, *args)
    r = run_bass_kernel_spmd(nc, [arrays], core_ids=[0])
    return r.results[0]["out_0"]
```

```python
from contextlib import ExitStack

import concourse.bass as bass
from concourse import mybir

F32 = mybir.dt.float32
I32 = mybir.dt.int32
BF16 = mybir.dt.bfloat16
F32R = mybir.dt.float32r
ALU = mybir.AluOpType
ACT = mybir.ActivationFunctionType
AX = mybir.AxisListType

B, S, H = 8, 56, 256
NH, HD = 16, 16
T = 1500
CH = 12
PAIRS = CH // 2
TP = T // CH
TPE = TP + TP % 2
PARTS = 3
CPP = CH // PARTS
TOK = B * S
NT = 4
TT = TOK // NT
KH = 2
HPH = NH // KH
HPG = HPH // 2
GR = HPG * HD
E, TOPK, F = 64, 6, 96
NG, TOPG = 8, 4
EPG = E // NG
CAP = 2 * (256 * TOPK // E)
SLOT = 64
SCALE = 2.5
GE = 4
GROUPS = E // GE
QUAD = 4
SW = 32
EARLY = NT - 1
LIMIT = 10000.0
EXP_MIN, EXP_MAX = 1.9287498479639178e-22, 5.184705528587072e21
EPS = 1e-5
TOP_SENTINEL, TAKEN = 3.0e38, -3.0e38
HUGE = 1.0e30


def build(nc, x, ctx_in, mask_in, Wq, bq, Wk, bk, Wv, bv, Wo, bo, gamma, beta, rs, gate_w, rbias,
          w_gate, w_up, w_down, ws_gate, ws_up, ws_down, out):
    with ExitStack() as st:
        def sb(name, shape, dt=F32):
            return st.enter_context(nc.sbuf_tensor(name, shape, dt))

        def sem(name):
            return st.enter_context(nc.semaphore(name))

        PS = st.enter_context(nc.psum_tensor("PS", [128, 8, 512], F32))

        ident = sb("ident", [128, 128])
        ident_b = sb("ident_b", [128, 128], BF16)
        head_mask = sb("head_mask", [128, HPG])
        before = sb("before", [TT, TT])
        ones = sb("ones", [TT, TT])
        slot_no = sb("slot_no", [TT, SLOT])
        x_sb = sb("x_sb", [TT, NT, H])
        w_raw = sb("w_raw", [128, 4, KH, H])
        bqk = sb("bqk", [128, 2, KH])
        bv_bc = sb("bv_bc", [128, H])
        bo_bc = sb("bo_bc", [TT, H])
        gamma_bc = sb("gamma_bc", [TT, H])
        beta_bc = sb("beta_bc", [TT, H])
        rbias_bc = sb("rbias_bc", [TT, E])
        rs_bc = sb("rs_bc", [TT, 1])
        mask_i = sb("mask_i", [TP, B, CH], I32)
        room = sb("room", [128, PARTS * CPP * H + 3 * NH * S + 4 * NH * (HD + 1)])
        room_r = sb("room_r", [128, 2 * NT * H + 2 * NT * GE * SLOT + 4 * TOK + 8 * H], F32R)
        used = [0, 0]

        def place(parts, pattern, rounded=False, **dims):
            size = 1
            for d in dims.values():
                size *= d
            at = used[rounded]
            used[rounded] += size
            return (room_r if rounded else room)[0:parts, at:at + size].rearrange(pattern, **dims)

        ctx_sb = place(TP, "p (j c d) -> p j c d", j=PARTS, c=CPP, d=H)
        v_sb = place(TP, "p (b h x) -> p b h x", b=4, h=NH, x=HD + 1)
        v_pair = v_sb.rearrange("p (n c) h x -> p n c h x", c=2)
        p_sb = place(TP, "p (b k q) -> p b k q", b=3, k=KH, q=HPH * S)
        gate_sb = sb("gate_sb", [128, KH, E])
        sg_sb = sb("sg_sb", [128, KH, F])
        su_sb = sb("su_sb", [128, KH, F])
        sd_sb = sb("sd_sb", [F, H])
        wgu_sb = sb("wgu_sb", [128, QUAD, GE, 2, KH, F])
        wd_sb = sb("wd_sb", [F, QUAD, GE, H])
        wT = sb("wT", [128, 2, KH, H])
        wkv_hi = sb("wkv_hi", [128, 2, KH, H], F32R)
        wkv_lo = sb("wkv_lo", [128, 2, KH, H], F32R)
        attend = sb("attend", [TP, B, CH])
        sc_scale = sb("sc_scale", [TP, B, CH])
        sc_bias = sb("sc_bias", [TP, B, CH])
        stats = sb("stats", [TT, NT, 6])
        mv = sb("mv", [TT, NT, 2])
        var_eps = sb("var_eps", [TT, NT])
        neg_half = sb("neg_half", [TT, NT])
        warm = sb("warm", [1, 1])
        rstd = sb("rstd", [TT, NT])
        xn = sb("xn", [TT, NT, H])
        xh = sb("xh", [TT, NT, H])
        clean_a = sb("clean_a", [128, NT * H])
        clean_m = sb("clean_m", [128, NT * H], I32)
        xT = sb("xT", [128, KH, TOK])
        q_raw = sb("q_raw", [128, KH, TOK])
        qT = sb("qT", [128, KH, TOK])
        q_hi = sb("q_hi", [128, KH, TOK], F32R)
        q_lo = sb("q_lo", [128, KH, TOK], F32R)
        q_bd = place(128, "p (b l k h s) -> p b l k h s", True, b=2, l=2, k=KH, h=HPH, s=S)
        cT_hi = place(128, "p (b k c t) -> p b k c t", True, b=2, k=KH, c=2, t=TPE)
        cT_lo = place(128, "p (b k c t) -> p b k c t", True, b=2, k=KH, c=2, t=TPE)
        k_split = place(128, "p (b j g t) -> p b j g t", True, b=2, j=KH, g=2, t=2 * TPE)
        kT = sb("kT", [128, KH, 2 * TPE])
        o_all = sb("o_all", [128, NT, B, S])
        den = sb("den", [TT, NT * NH])
        rden = sb("rden", [TT, NT * NH])
        psum_p = sb("psum_p", [TT, NT * NH])
        o_tok = q_raw[0:TT].rearrange("p k t -> p (k t)")[:, 0:EARLY * NH * (HD + 1)].rearrange(
            "p (i h x) -> p i h x", i=EARLY, h=NH)
        ao = sb("ao", [TT, NT, H])
        delta = sb("delta", [TT, NT, H])
        x1 = sb("x1", [TT, NT, H])
        neg = sb("neg", [TT, NT, E])
        score = sb("score", [TT, NT, E])
        biased = sb("biased", [TT, NT, E])
        top_g = sb("top_g", [TT, NT, NG, 8])
        gsc = sb("gsc", [TT, NT, NG + 8])
        top8 = sb("top8", [TT, NT, 8])
        g_left = sb("g_left", [TT, NT, NG + 8])
        g_pick = sb("g_pick", [TT, NT, NG])
        cand = sb("cand", [TT, NT, E + 8])
        e_left = sb("e_left", [TT, NT, E + 8])
        pick = sb("pick", [TT, NT, E])
        wsum = sb("wsum", [TT, NT])
        wtok = sb("wtok", [TT, NT, E])
        slot = sb("slot", [TT, NT, E])
        used = [0, 0]
        xn_hi = place(TT, "p (i d) -> p i d", True, i=NT, d=H)
        xn_lo = place(TT, "p (i d) -> p i d", True, i=NT, d=H)
        put = place(TT, "p (b i e s) -> p b i e s", True, b=2, i=NT, e=GE, s=SLOT)
        putT = place(128, "p (b c t) -> p b c t", True, b=2, c=2, t=TOK)
        eo_hi = place(128, "p (b c d) -> p b c d", True, b=2, c=2, d=H)
        eo_lo = place(128, "p (b c d) -> p b c d", True, b=2, c=2, d=H)
        put_b = place(TT, "p (b x) -> p b x", b=2, x=NT * GE * SLOT // 2).bitcast(BF16).rearrange(
            "p b (i x) -> p b i x", i=NT)
        act_g = place(128, "p (b c f) -> p b c f", b=2, c=2, f=F)
        h_sb = place(128, "p (b c f) -> p b c f", b=2, c=2, f=F)
        hT = place(F, "p (b x) -> p b x", b=2, x=GE * SLOT)
        bufT = sb("bufT", [128, 2, KH, GE, SLOT])
        w3 = place(TT, "p (i x) -> p i x", i=NT, x=E * 3 // 2).bitcast(BF16).rearrange("p i (e w) -> p i e w", w=3)
        w_rest = neg
        slot_w = sb("slot_w", [128, 2, 2])
        sh_g, sh_h = q_raw[0:F, 0, :], qT[0:F, 0, :]
        y_sb = xh

        x_first_in, x_in, b_in, mask_in_s, small_in = sem("x_first_in"), sem("x_in"), sem("b_in"), sem("mask_in"), sem("small_in")
        w_in = [sem(f"w_in{w}") for w in range(4)]
        ctx_loaded = [sem(f"ctx_loaded{j}") for j in range(PARTS)]
        ew_loaded = [sem(f"ew_loaded{j}") for j in range(QUAD)]
        out_done = sem("out_done")
        pool_step, dve_step = sem("pool_step"), sem("dve_step")
        ident_ready, pads_ready, consts = sem("ident_ready"), sem("pads_ready"), sem("consts")
        var_ready, rstd_ready = sem("var_ready"), sem("rstd_ready")
        wT_psum, wT_ready, w_lo_ready = sem("wT_psum"), sem("wT_ready"), sem("w_lo_ready")
        xn_ready, xh_ready, xT_psum, xT_ready = sem("xn_ready"), sem("xh_ready"), sem("xT_psum"), sem("xT_ready")
        q_psum, q_saved, qT_ready = sem("q_psum"), sem("q_saved"), sem("qT_ready")
        q_first_ready, qbd_ready, mask_ready = sem("q_first_ready"), sem("qbd_ready"), sem("mask_ready")
        cT_psum, cT_hi_ready, cT_ready = sem("cT_psum"), sem("cT_hi_ready"), sem("cT_ready")
        k_psum, kv_psum, k_raw, k_hi_ready, kT_ready, v_ready = (sem("k_psum"), sem("kv_psum"), sem("k_raw"), sem("k_hi_ready"),
                                                         sem("kT_ready"), sem("v_ready"))
        s_psum, exp_done, p_ready, pv_done, o_saved = (sem("s_psum"), sem("exp_done"), sem("p_ready"),
                                                       sem("pv_done"), sem("o_saved"))
        oT_psum, oT_saved, ao_ready, aoT_psum, aoT_ready = (sem("oT_psum"), sem("oT_saved"), sem("ao_ready"),
                                                            sem("aoT_psum"), sem("aoT_ready"))
        od_psum, od_saved, bounds_ready, xb_ready = sem("od_psum"), sem("od_saved"), sem("bounds_ready"), sem("xb_ready")
        logit_psum, neg_ready = sem("logit_psum"), sem("neg_ready")
        sh_psum, shg_ready, shh_ready = sem("sh_psum"), sem("shg_ready"), sem("shh_ready")
        pick_ready, pos_psum, w3_ready = sem("pick_ready"), sem("pos_psum"), sem("w3_ready")
        slot_ready, put_early_ready = sem("slot_ready"), sem("put_early_ready")
        xn_hi_ready, xs_ready = sem("xn_hi_ready"), sem("xs_ready")
        put_ready, putb_ready = sem("put_ready"), sem("putb_ready")
        buf_psum, buf_ready = sem("buf_psum"), sem("buf_ready")
        gu_psum, actg_ready, sw_ready, h_ready = sem("gu_psum"), sem("actg_ready"), sem("sw_ready"), sem("h_ready")
        hT_psum, hT_ready = sem("hT_psum"), sem("hT_ready")
        z_psum, z_saved, eo_ready = sem("z_psum"), sem("z_saved"), sem("eo_ready")
        combined = sem("combined")
        y_ready = sem("y_ready")

        block = st.enter_context(nc.Block())

        turned_bank = PS[:, 0, 0:KH * 2 * TP].rearrange("p (k c t) -> p k c t", k=KH, c=2)
        key_bank = PS[:, 1, 0:KH * 2 * TPE].rearrange("p (j t) -> p j t", j=KH)
        value_bank = PS[0:TP, 2, :].rearrange("p (c d) -> p c d", c=2)

        spare = PS[:, 0:3:2, :]
        first_pair = PS[:, 6:8, :]

        lower, upper = slice(0, GR), slice(GR, 2 * GR)

        def score_banks(n):
            return PS[0:TP, 3 + 2 * (n % 2):5 + 2 * (n % 2), 0:HPH * S]

        def y_bank(i):
            return PS[0:TT, i // 2, (i % 2) * H:(i % 2 + 1) * H]

        buf_banks = PS[:, 2:4, 0:2 * GE * CAP].rearrange("p k (g e s) -> p k g e s", g=2, e=GE)

        gu_bank = PS[:, 4, 0:4 * F].rearrange("p (c u f) -> p c u f", c=2, u=2)
        sw_bank = PS[:, 4, 4 * F:4 * F + 12].rearrange("p (c e w) -> p c e w", c=2, e=2)
        hT_bank = PS[0:F, 5, 0:GE * SLOT]

        def after(eng, s, value):
            if isinstance(value, int) and value <= 0:
                return
            eng.wait_ge(s, value)

        ctx_v = ctx_in.rearrange("b (p c) d -> b p c d", c=CH)
        x_v = x.rearrange("b s d -> (b s) d").rearrange("(i p) d -> p i d", p=TT)
        out_v = out.rearrange("b s d -> (b s) d").rearrange("(i p) d -> p i d", p=TT)
        wg_v = w_gate.rearrange("e (p k) f -> p e k f", k=KH)
        wu_v = w_up.rearrange("e (p k) f -> p e k f", k=KH)
        wd_v = w_down.rearrange("e f d -> f e d")

        @block.sync
        def _(sp):
            def load_ctx(b, j):
                sp.dma_start(ctx_sb[:, j], ctx_v[b, :, j * CPP:(j + 1) * CPP, :]).then_inc(ctx_loaded[j], 16)

            def load_experts(g, c):
                for u, w in enumerate((wg_v, wu_v)):
                    sp.dma_start(wgu_sb[:, c, :, u], w[:, bass.ds(g * GE, GE)]).then_inc(ew_loaded[c], 16)
                sp.dma_start(wd_sb[:, c], wd_v[:, bass.ds(g * GE, GE)]).then_inc(ew_loaded[c], 16)

            def load_weight(w, src):
                sp.dma_start(w_raw[:, w], src.rearrange("(o p) k -> p o k", p=128)).then_inc(w_in[w], 16)

            sp.dma_start(x_sb[:, 0:1], x_v[:, 0:1]).then_inc(x_first_in, 16)
            load_weight(0, Wq)
            load_weight(1, Wk)
            load_ctx(0, 0)
            load_weight(2, Wv)
            sp.dma_start(x_sb[:, 1:NT], x_v[:, 1:NT]).then_inc(x_in, 16)
            load_ctx(0, 1)
            load_ctx(0, 2)
            load_weight(3, Wo)
            small = ((bo_bc, bo), (gamma_bc, gamma), (beta_bc, beta), (rbias_bc, rbias), (rs_bc, rs))
            for dst, src in small:
                sp.dma_start(dst[:], src.partition_broadcast(TT)).then_inc(small_in, 16)
            sp.dma_start(gate_sb[:], gate_w.rearrange("(k p) e -> p k e", p=128)).then_inc(small_in, 16)
            sp.dma_start(sg_sb[:], ws_gate.rearrange("(k p) e -> p k e", p=128)).then_inc(small_in, 16)
            sp.dma_start(su_sb[:], ws_up.rearrange("(k p) e -> p k e", p=128)).then_inc(small_in, 16)
            sp.dma_start(sd_sb[:], ws_down).then_inc(small_in, 16)
            for c in range(QUAD):
                load_experts(c, c)

            with sp.Fori(1, B) as b:
                for j in range(PARTS):
                    sp.wait_ge(cT_psum, b * PAIRS - PAIRS + (j + 1) * CPP // 2)
                    load_ctx(b, j)
            with sp.Fori(1, GROUPS // QUAD) as q:
                for c in range(QUAD):
                    sp.wait_ge(z_psum, (q * QUAD - QUAD + c + 1) * 3)
                    load_experts(q * QUAD + c, c)
            for i in range(2):
                sp.wait_ge(y_ready, i + 1)
                sp.dma_start(out_v[:, 2 * i:2 * i + 2], y_sb[:, 2 * i:2 * i + 2]).then_inc(out_done, 16)
            sp.wait_ge(out_done, 32)

        @block.gpsimd
        def _(pool):
            done = [0]

            def step(ins):
                done[0] += 1
                ins.then_inc(pool_step, 1)
                pool.wait_ge(pool_step, done[0])

            step(nc.gpsimd.memset(ident[:], 0.0))
            nc.gpsimd.affine_select(out=ident[:], in_=ident[:], compare_op=ALU.not_equal, fill=1.0, base=0,
                                    pattern=[[-1, 128]], channel_multiplier=1).then_inc(ident_ready, 1)
            step(nc.gpsimd.memset(neg_half[:], -0.5))
            nc.gpsimd.memset(cT_hi[:, :, :, :, TP:TPE].bitcast(F32), 0.0)
            nc.gpsimd.memset(cT_lo[:, :, :, :, TP:TPE].bitcast(F32), 0.0)
            step(nc.gpsimd.memset(head_mask[:], 1.0))
            for rows in (lower, upper):
                step(nc.gpsimd.affine_select(out=head_mask[rows], in_=head_mask[rows], compare_op=ALU.is_ge, fill=0.0,
                                             base=0, pattern=[[-HD, HPG]], channel_multiplier=1))
                step(nc.gpsimd.affine_select(out=head_mask[rows], in_=head_mask[rows], compare_op=ALU.is_ge, fill=0.0,
                                             base=HD - 1, pattern=[[HD, HPG]], channel_multiplier=-1))
            nc.gpsimd.memset(v_sb[:, :, :, HD:], 1.0).then_inc(pads_ready, 1)

            def inverse_roots(i0, i1, count):
                pool.wait_ge(var_ready, count)
                nc.gpsimd.tensor_tensor(rstd[:, i0:i1], var_eps[:, i0:i1], neg_half[:, i0:i1], ALU.pow).then_inc(rstd_ready, 1)

            inverse_roots(0, 1, 1)
            pool.wait_ge(ident_ready, 1)
            nc.gpsimd.tensor_copy(ident_b[:], ident[:])
            step(nc.gpsimd.memset(before[:], 1.0))
            step(nc.gpsimd.affine_select(out=before[:], in_=before[:], compare_op=ALU.is_ge, fill=0.0, base=-1,
                                         pattern=[[1, TT]], channel_multiplier=-1))

            def place_queries(b, halves=(0, 1), parts=4):
                for half in halves:
                    for group, rows in enumerate((lower, upper)):
                        for t, to in enumerate((lower, upper)[:parts - group * 2]):
                            nc.gpsimd.tensor_tensor(
                                q_bd[to, b % 2, half, :, group * HPG:(group + 1) * HPG],
                                (q_hi, q_lo)[half][rows, :, bass.ds(b * S, S)].bitcast(F32).unsqueeze(2).to_broadcast([GR, KH, HPG, S]),
                                head_mask[rows].unsqueeze(1).unsqueeze(3).to_broadcast([GR, KH, HPG, S]),
                                ALU.mult).then_inc(qbd_ready, 1)
                            pool.wait_ge(qbd_ready, b * 8 + half * 4 + group * 2 + t - (4 if parts == 4 else 3))

            pool.wait_ge(qT_ready, 1)
            place_queries(0, (1,), 3)
            place_queries(1)
            nc.gpsimd.memset(bufT[:], 0.0)
            nc.gpsimd.memset(ones[:], 1.0)
            nc.gpsimd.memset(slot_no[:], -1.0).then_inc(consts, 1)
            pool.wait_ge(consts, 1)
            nc.gpsimd.iota(slot_no[:, 0:CAP], pattern=[[1, CAP]], base=1, channel_multiplier=0,
                           allow_small_or_imprecise_dtypes=True).then_inc(consts, 1)
            inverse_roots(1, NT, 2)

            def bounded(dst, src, a, count):
                nc.gpsimd.tensor_scalar(a, src, 0.0, LIMIT, ALU.max, ALU.min).then_inc(bounds_ready, 1)
                nc.gpsimd.tensor_scalar(dst, src, 0.0, -LIMIT, ALU.min, ALU.max).then_inc(bounds_ready, 1)
                pool.wait_ge(bounds_ready, count + 2)
                nc.gpsimd.tensor_tensor(dst, dst, a, ALU.add).then_inc(bounds_ready, 1)

            pool.wait_ge(xn_ready, 1)
            later_input = (t[:, 1:NT].rearrange("p i d -> p (i d)") for t in (xh, xn))
            bounded(*later_input, clean_a[0:TT, 0:EARLY * H], 0)
            pool.wait_ge(q_saved, 2 * KH)
            bounded(qT[:, :, 0:EARLY * TT], q_raw[:, :, 0:EARLY * TT],
                    clean_a[:, 0:KH * EARLY * TT].rearrange("p (k c) -> p k c", k=KH), 3)
            pool.wait_ge(qT_ready, 2)
            pool.wait_ge(small_in, 9 * 16)
            nc.gpsimd.tensor_tensor(x_sb[:], x_sb[:], beta_bc[:].unsqueeze(1).to_broadcast([TT, NT, H]), ALU.add
                                    ).then_inc(xb_ready, 1)
            with pool.Fori(2, B) as b:
                pool.wait_ge(s_psum, b * CH - CH)
                place_queries(b)

            pool.wait_ge(od_saved, 2)
            early_delta = (t[:, 0:EARLY].rearrange("p i d -> p (i d)") for t in (delta, xn))
            bounded(*early_delta, clean_a[0:TT, 0:EARLY * H], 6)
            inverse_roots(0, EARLY, 3)
            inverse_roots(0, EARLY, 4)

            def token_rest(i0, i1, count):
                pool.wait_ge(xn_hi_ready, count)
                nc.gpsimd.tensor_tensor(xn_lo[:, i0:i1], xn[:, i0:i1], xn_hi[:, i0:i1].bitcast(F32),
                                        ALU.subtract).then_inc(xs_ready, 1)

            token_rest(0, EARLY, 1)
            inverse_roots(EARLY, NT, 5)
            inverse_roots(EARLY, NT, 6)
            token_rest(EARLY, NT, 2)

            def narrow(g, c):
                pool.wait_ge(put_ready, g + 1)
                after(pool, z_psum, (g - 2) * 3 + 2)
                after(pool, gu_psum, g - 1)
                p = put[:, c % 2].bitcast(F32).rearrange("p i e s -> p i (e s)")
                nc.gpsimd.tensor_tensor(put_b[:, c % 2], p, p, ALU.mult).then_inc(putb_ready, 1)

            for c in range(QUAD):
                narrow(c, c)
            with pool.Fori(1, GROUPS // QUAD) as q:
                for c in range(QUAD):
                    narrow(q * QUAD + c, c)

        @block.scalar
        def _(act):
            act.dma_start(bqk[:, 0], bq.rearrange("(j p) -> p j", p=128), allow_slow_non_contiguous=True).then_inc(b_in, 16)
            act.dma_start(bqk[:, 1], bk.rearrange("(j p) -> p j", p=128), allow_slow_non_contiguous=True).then_inc(b_in, 16)
            act.dma_start(bv_bc[:], bv.partition_broadcast(128)).then_inc(b_in, 16)
            act.dma_start(mask_i[:], mask_in.rearrange("b (p c) -> p b c", c=CH)).then_inc(mask_in_s, 16)

            act.wait_ge(ident_ready, 1)
            nc.scalar.activation(warm[:], ident[0:1, 0:1], ACT.Exp)

            def weight_in(w, dst):
                act.wait_ge(wT_psum, w + 1)
                nc.scalar.copy(dst, PS[:, 3 + w % 3, :].rearrange("p (k o) -> p k o", k=KH)).then_inc(wT_ready, 1)

            def turned_rows(i0, i1, banks, psum, count, ready):
                act.wait_ge(psum, count)
                for k in range(KH):
                    nc.scalar.copy(xT[:, k, i0 * TT:i1 * TT], banks[:, k, 0:(i1 - i0) * TT]).then_inc(ready, 1)

            def exp_logits(i0, i1, count):
                act.wait_ge(logit_psum, count)
                nc.scalar.activation(neg[:, i0:i1], PS[0:TT, 0, i0 * E:i1 * E].rearrange("p (i e) -> p i e", i=i1 - i0),
                                     ACT.Exp, scale=-1.0).then_inc(neg_ready, 1)

            def context_hi(n, m):
                act.wait_ge(cT_psum, n + 1)
                after(act, kv_psum, n - 1)
                nc.scalar.copy(cT_hi[:, m % 2, :, :, 0:TP], turned_bank).then_inc(cT_hi_ready, 1)

            def keys_hi(n, m):
                act.wait_ge(k_raw, n + 1)
                after(act, s_psum, n * 2 - 2)
                for group, rows in enumerate((lower, upper)):
                    nc.scalar.copy(k_split[rows, m % 2, :, group], kT[rows]).then_inc(k_hi_ready, 1)

            def exps(n, b, c):
                act.wait_ge(s_psum, n + 1)
                after(act, pv_done, n - 2)
                nc.scalar.activation(p_sb[:, c % 3], score_banks(c), ACT.Exp, bias=sc_bias[:, b, c:c + 1],
                                     scale=sc_scale[:, b, c:c + 1]).then_inc(exp_done, 1)

            def nothing(u):
                pass

            def queries_beside(u):
                if u == 5:
                    turned_rows(1, NT, spare, xT_psum, 2, xT_ready)

            def rest_beside(u):
                if u in (0, 1):
                    act.wait_ge(oT_psum, u + 1)
                    for r, i in enumerate(((0, 1), (2,))[u]):
                        nc.scalar.copy(o_tok[:, i], spare[0:TT, r].rearrange("p (h x) -> p h x", x=SW)[:, :, 0:HD + 1]
                                       ).then_inc(oT_saved, 1)
                if u == 9:
                    turned_rows(0, EARLY, spare, xT_psum, 3, xT_ready)
                if u == 10:
                    exp_logits(0, EARLY, 1)

            def rest_midway(u):
                if u == 2:
                    turned_rows(0, EARLY, spare, aoT_psum, 1, aoT_ready)

            def batch(b, last, beside=nothing, midway=nothing, before_it=0):
                for m in range(PAIRS):
                    n = b * PAIRS + m
                    exps(n * 2, b, 2 * m)
                    beside(before_it + m)
                    if m + 1 < PAIRS or not last:
                        keys_hi(n + 1, m + 1)
                    exps(n * 2 + 1, b, 2 * m + 1)
                    midway(before_it + m)
                    if m + 2 < PAIRS or not last:
                        context_hi(n + 2, m + 2)

            weight_in(0, wT[:, 0])
            weight_in(1, wkv_hi[:, 0])
            turned_rows(0, 1, first_pair, xT_psum, 1, xT_ready)
            context_hi(0, 0)
            weight_in(2, wkv_hi[:, 1])
            context_hi(1, 1)
            weight_in(3, wT[:, 1])
            keys_hi(0, 0)
            act.wait_ge(mask_ready, 1)
            batch(0, False, queries_beside, nothing, 0)
            batch(1, False, queries_beside, nothing, PAIRS)
            with act.Fori(2, B - 2) as b:
                batch(b, False)
            batch(B - 2, False, rest_beside, rest_midway, 0)
            batch(B - 1, True, rest_beside, rest_midway, PAIRS)

            def token_hi(i0, i1, count):
                act.wait_ge(xh_ready, count)
                nc.scalar.copy(xn_hi[:, i0:i1], xn[:, i0:i1]).then_inc(xn_hi_ready, 1)

            token_hi(0, EARLY, 3)
            turned_rows(EARLY, NT, spare, aoT_psum, 2, aoT_ready)
            turned_rows(EARLY, NT, spare, xT_psum, 4, xT_ready)
            token_hi(EARLY, NT, 4)
            exp_logits(EARLY, NT, 2)
            act.wait_ge(sh_psum, 2)
            nc.scalar.activation(sh_g, PS[0:F, 3, 0:TOK], ACT.Silu).then_inc(shg_ready, 1)

            def group(g, c):
                act.wait_ge(gu_psum, g + 1)
                after(act, h_ready, (g - 1) * 2)
                nc.scalar.activation(act_g[:, c % 2], gu_bank[:, :, 0, :], ACT.Silu).then_inc(actg_ready, 1)
                after(act, combined, (g - 1) * 2)
                for p in range(2):
                    act.wait_ge(z_psum, g * 3 + p + 1)
                    nc.scalar.copy(putT[:, c % 2, p], PS[:, 6 + (3 * c + p) % 2, 0:TOK // 2].bitcast(BF16)
                                   ).then_inc(z_saved, 1)
                act.wait_ge(hT_psum, g + 1)
                after(act, z_psum, (g - 1) * 3)
                nc.scalar.copy(hT[:, c % 2], hT_bank).then_inc(hT_ready, 1)
                act.wait_ge(z_psum, g * 3 + 3)
                nc.scalar.copy(eo_hi[:, c % 2], PS[:, 6 + (3 * c + 2) % 2, :].rearrange("p (k d) -> p k d", k=2)
                               ).then_inc(z_saved, 1)

            for c in range(QUAD):
                group(c, c)
            with act.Fori(1, GROUPS // QUAD) as q:
                for c in range(QUAD):
                    group(q * QUAD + c, c)

        @block.vector
        def _(dve):
            done = [0]

            def step(ins):
                done[0] += 1
                ins.then_inc(dve_step, 1)
                dve.wait_ge(dve_step, done[0])

            def finite(m, src):
                step(nc.vector.tensor_scalar(m, src, 0.0, 0.0, ALU.mult, ALU.is_equal))

            def clean(dst, src, a, m, ready=None):
                nc.vector.tensor_scalar(m, src, 0.0, 0.0, ALU.mult, ALU.is_equal)
                nc.vector.tensor_scalar(a, src, 0.0, LIMIT, ALU.max, ALU.min)
                step(nc.vector.tensor_scalar(dst, src, 0.0, -LIMIT, ALU.min, ALU.max))
                step(nc.vector.tensor_tensor(dst, dst, a, ALU.add))
                ins = nc.vector.copy_predicated(dst, m, src)
                if ready is None:
                    step(ins)
                else:
                    ins.then_inc(ready, 1)

            def add_delta(i0, i1, count):
                for i in range(i0, i1):
                    ins = nc.vector.scalar_tensor_tensor(out=xn[:, i], in0=delta[:, i], scalar=mv[:, i, 0:1], in1=gamma_bc[:],
                                                         op0=ALU.subtract, op1=ALU.mult)
                step(ins)
                dve.wait_ge(xb_ready, 1)
                dve.wait_ge(rstd_ready, count)
                for i in range(i0, i1):
                    ins = nc.vector.scalar_tensor_tensor(out=x1[:, i], in0=xn[:, i], scalar=rstd[:, i:i + 1], in1=x_sb[:, i],
                                                         op0=ALU.mult, op1=ALU.add)
                step(ins)

            def moments(i0, i1, src):
                for i in range(i0, i1):
                    ins = nc.vector.bn_stats(stats[:, i], src[:, i])
                step(ins)
                for i in range(i0, i1):
                    ins = nc.vector.bn_aggr(mv[:, i], stats[:, i])
                step(ins)
                nc.vector.tensor_scalar(var_eps[:, i0:i1], mv[:, i0:i1, 1], EPS, None, ALU.add).then_inc(var_ready, 1)

            def normalise(i0, i1, dst, src, count, ready=None):
                dve.wait_ge(rstd_ready, count)
                for i in range(i0, i1):
                    ins = nc.vector.tensor_scalar(dst[:, i], src[:, i], mv[:, i, 0:1], rstd[:, i:i + 1],
                                                  ALU.subtract, ALU.mult)
                if ready is None:
                    step(ins)
                else:
                    ins.then_inc(ready, 1)

            def flat(t):
                return t.rearrange("p i d -> p (i d)")

            nc.vector.memset(gsc[:, :, NG:], TOP_SENTINEL)
            nc.vector.memset(cand[:, :, E:], TOP_SENTINEL)
            dve.wait_ge(x_first_in, 16)
            moments(0, 1, x_sb)
            normalise(0, 1, xn, x_sb, 1)
            clean(xh[:, 0], xn[:, 0], clean_a[0:TT, 0:H], clean_m[0:TT, 0:H], xh_ready)

            def weight_lo(w):
                dve.wait_ge(wT_ready, w + 2)
                nc.vector.tensor_tensor(wkv_lo[:, w], PS[:, 4 + w, :].rearrange("p (k o) -> p k o", k=KH),
                                        wkv_hi[:, w].bitcast(F32), ALU.subtract).then_inc(w_lo_ready, 1)

            weight_lo(0)
            dve.wait_ge(mask_in_s, 16)
            step(nc.vector.tensor_copy(attend[:], mask_i[:]))
            step(nc.vector.tensor_scalar(attend[:], attend[:], 0.5, None, ALU.is_gt))
            step(nc.vector.tensor_scalar(sc_scale[:], attend[:], 1.0 / HD ** 0.5, None, ALU.mult))
            nc.vector.tensor_scalar(sc_bias[:], attend[:], 50.0, -50.0, ALU.mult, ALU.add).then_inc(mask_ready, 1)
            dve.wait_ge(b_in, 48)

            def context_lo(n, m):
                dve.wait_ge(cT_hi_ready, n + 1)
                after(dve, kv_psum, n - 1)
                nc.vector.tensor_tensor(cT_lo[:, m % 2, :, :, 0:TP], turned_bank,
                                        cT_hi[:, m % 2, :, :, 0:TP].bitcast(F32), ALU.subtract).then_inc(cT_ready, 1)

            def keys(n, m):
                dve.wait_ge(k_psum, n + 1)
                after(dve, kT_ready, n * 2)
                nc.vector.tensor_tensor(kT[:], key_bank, bqk[:, 1].unsqueeze(2).to_broadcast([128, KH, 2 * TPE]),
                                        ALU.add).then_inc(k_raw, 1)

            def keys_lo(n, m):
                after(dve, s_psum, n * 2 - 2)
                for group, (rows, to) in enumerate(((lower, upper), (upper, lower))):
                    dve.wait_ge(k_hi_ready, n * 2 + group + 1)
                    nc.vector.tensor_tensor(k_split[to, m % 2, :, group], kT[rows], k_split[rows, m % 2, :, group].bitcast(F32),
                                            ALU.subtract).then_inc(kT_ready, 1)

            def values(n, m):
                dve.wait_ge(kv_psum, n + 1)
                after(dve, pv_done, n * 2 - 2)
                nc.vector.tensor_tensor(
                    v_pair[:, m % 2, :, :, 0:HD], value_bank.rearrange("p c (h d) -> p (c h) d", d=HD).rearrange("p (c h) d -> p c h d", c=2),
                    bv_bc[0:TP].rearrange("p (h d) -> p h d", h=NH).unsqueeze(1).to_broadcast([TP, 2, NH, HD]),
                    ALU.add).then_inc(v_ready, 1)

            def clip(n, c):
                dve.wait_ge(exp_done, n + 1)
                nc.vector.tensor_scalar(p_sb[:, c % 3], p_sb[:, c % 3], EXP_MIN, EXP_MAX, ALU.max, ALU.min).then_inc(p_ready, 1)

            def sigmoids(i0, i1, count):
                n, tiles = i1 - i0, slice(i0, i1)
                dve.wait_ge(neg_ready, count)
                step(nc.vector.tensor_scalar(neg[:, tiles], neg[:, tiles], 1.0, None, ALU.add))
                step(nc.vector.reciprocal(score[:, tiles], neg[:, tiles]))
                step(nc.vector.tensor_tensor(biased[:, tiles], score[:, tiles], rbias_bc[:].unsqueeze(1).to_broadcast([TT, n, E]), ALU.add))

            def group_bests(i0, i1):
                for i in range(i0, i1):
                    for k in range(NG):
                        ins = nc.vector.max(top_g[:, i, k], biased[:, i, k * EPG:(k + 1) * EPG])
                step(ins)

            def pick_groups(i0, i1):
                tiles = slice(i0, i1)
                step(nc.vector.tensor_tensor(gsc[:, tiles, 0:NG], top_g[:, tiles, :, 0], top_g[:, tiles, :, 1], ALU.add))
                first_best(i0, i1, gsc, g_left, NG, TOPG)
                step(nc.vector.tensor_scalar(g_pick[:, tiles], g_left[:, tiles, 0:NG], TAKEN, HUGE, ALU.is_equal, ALU.mult))

            def first_best(i0, i1, values, left, width, count):
                for i in range(i0, i1):
                    ins = nc.vector.max(top8[:, i], values[:, i, 0:width])
                step(ins)
                step(nc.vector.memset(top8[:, i0:i1, count:8], TOP_SENTINEL))
                for i in range(i0, i1):
                    ins = nc.vector.match_replace(left[:, i], top8[:, i], values[:, i], TAKEN)
                step(ins)

            def route_experts(i0, i1):
                tiles = slice(i0, i1)
                for i in range(i0, i1):
                    ins = nc.vector.scalar_tensor_tensor(
                        out=cand[:, i, 0:E].rearrange("p (k e) -> p k e", k=NG), in0=g_pick[:, i].unsqueeze(2).to_broadcast([TT, NG, EPG]),
                        scalar=-HUGE, in1=biased[:, i].rearrange("p (k e) -> p k e", k=NG), op0=ALU.add, op1=ALU.add)
                step(ins)
                first_best(i0, i1, cand, e_left, E, TOPK)
                nc.vector.tensor_scalar(pick[:, tiles], e_left[:, tiles, 0:E], TAKEN, None, ALU.is_equal).then_inc(pick_ready, 1)

            def token_weights(i0, i1, count):
                n = i1 - i0
                sc, pk, wt, ws = (t[:, i0:i1] for t in (score, pick, wtok, wsum))
                dve.wait_ge(pick_ready, count)
                step(nc.vector.tensor_tensor(wt, sc, pk, ALU.mult))
                step(nc.vector.tensor_reduce(ws, wt, AX.X, ALU.add))
                step(nc.vector.reciprocal(ws, ws))
                step(nc.vector.tensor_tensor(wt, wt, ws.unsqueeze(2).to_broadcast([TT, n, E]), ALU.mult))
                step(nc.vector.tensor_scalar(wt, wt, SCALE, None, ALU.mult))

            def weight_parts(i0, i1, ready):
                rest, left, parts = wtok[:, i0:i1], w_rest[:, i0:i1], w3[:, i0:i1]
                for part in range(3):
                    ins = nc.vector.tensor_copy(parts[:, :, :, part], rest)
                    if part == 2:
                        ins.then_inc(ready, 1)
                    else:
                        step(ins)
                        step(nc.vector.tensor_tensor(left, rest, parts[:, :, :, part], ALU.subtract))
                        rest = left

            def token_slots(i0, i1, count):
                dve.wait_ge(pos_psum, count)
                pos = PS[0:TT, 7 - i0 // EARLY, i0 * E:i1 * E].rearrange("p (i e) -> p i e", i=i1 - i0)
                nc.vector.scalar_tensor_tensor(out=slot[:, i0:i1], in0=pos, scalar=1.0, in1=pick[:, i0:i1],
                                               op0=ALU.add, op1=ALU.mult).then_inc(slot_ready, 1)

            def first_routes(i0, i1, c):
                dve.wait_ge(slot_ready, 1 + i0 // EARLY)
                nc.vector.tensor_tensor(
                    put[:, c, i0:i1], slot_no[:].unsqueeze(1).unsqueeze(1).to_broadcast([TT, i1 - i0, GE, SLOT]),
                    slot[:, i0:i1, c * GE:(c + 1) * GE].unsqueeze(3).to_broadcast([TT, i1 - i0, GE, SLOT]),
                    ALU.is_equal).then_inc(put_ready if i0 else put_early_ready, 1)

            def queries_saved(i0, i1, banks, count):
                dve.wait_ge(q_psum, count)
                for j in range(KH):
                    nc.vector.tensor_scalar(q_raw[:, j, 0:(i1 - i0) * TT], banks[:, j, 0:(i1 - i0) * TT],
                                                  bqk[:, 0, j:j + 1], None, ALU.add).then_inc(q_saved, 1)
                dve.wait_ge(q_saved, KH * count)

            def queries_split(i0, i1):
                cols = slice(i0 * TT, i1 * TT)
                step(nc.vector.tensor_copy(q_hi[:, :, cols], qT[:, :, 0:(i1 - i0) * TT]))
                nc.vector.tensor_tensor(q_lo[:, :, cols], qT[:, :, 0:(i1 - i0) * TT], q_hi[:, :, cols].bitcast(F32),
                                        ALU.subtract).then_inc(qT_ready, 1)

            def attention_output(i0, i1, heads):
                d, r, p = (t[:, i0 * NH:i1 * NH] for t in (den, rden, psum_p))
                step(nc.vector.tensor_copy(d, heads[:, :, HD]))
                step(nc.vector.reciprocal(r, d))
                step(nc.vector.tensor_tensor(p, d, r, ALU.mult))
                step(nc.vector.scalar_tensor_tensor(out=p, in0=p, scalar=1e-8, in1=d, op0=ALU.add, op1=ALU.mult))
                step(nc.vector.reciprocal(r, p))
                nc.vector.tensor_tensor(ao[:, i0:i1].rearrange("p i (h d) -> p (i h) d", d=HD), heads[:, :, 0:HD],
                                        r.unsqueeze(2).to_broadcast([TT, (i1 - i0) * NH, HD]), ALU.mult).then_inc(ao_ready, 1)

            def delta_saved(i0, i1, count):
                dve.wait_ge(od_psum, count)
                for r in range(0, i1 - i0, 2):
                    w = min(2, i1 - i0 - r)
                    nc.vector.tensor_tensor(
                        xn[:, i0 + r:i0 + r + w], spare[0:TT, r // 2, 0:w * H].rearrange("p (i d) -> p i d", i=w),
                        bo_bc[:].unsqueeze(1).to_broadcast([TT, w, H]), ALU.add).then_inc(od_saved, 1)

            def nothing(u):
                pass

            def queries_beside(u):
                if u == 6:
                    queries_saved(1, NT, spare, 2)

            def queries_between(u):
                later = ((flat(xh[:, 1:NT]), flat(xn[:, 1:NT])), (qT[:, :, 0:EARLY * TT], q_raw[:, :, 0:EARLY * TT]))
                later_m = clean_m[:, 0:KH * EARLY * TT].rearrange("p (k c) -> p k c", k=KH)
                if u == 0:
                    dve.wait_ge(x_in, 16)
                    moments(1, NT, x_sb)
                if u == 1:
                    normalise(1, NT, xn, x_sb, 2, xn_ready)
                if u == 2:
                    dve.wait_ge(xn_ready, 1)
                    finite(clean_m[0:TT, 0:EARLY * H], later[0][1])
                if u == 3:
                    dve.wait_ge(bounds_ready, 3)
                    nc.vector.copy_predicated(later[0][0], clean_m[0:TT, 0:EARLY * H], later[0][1]).then_inc(xh_ready, 1)
                if u == 6:
                    finite(later_m, later[1][1])
                if u == 7:
                    dve.wait_ge(bounds_ready, 6)
                    step(nc.vector.copy_predicated(later[1][0], later_m, later[1][1]))
                if u == 8:
                    queries_split(1, NT)

            def rest_beside(u):
                if u == 3:
                    delta_saved(0, EARLY, 1)
                if u == 11:
                    group_bests(0, 1)

            def rest_between(u):
                d, n = flat(delta[:, 0:EARLY]), flat(xn[:, 0:EARLY])
                if u in (0, 1):
                    tiles = ((0, 2), (2, EARLY))[u]
                    dve.wait_ge(oT_saved, tiles[1])
                    attention_output(*tiles, o_tok[:, tiles[0]:tiles[1]].rearrange("p i h x -> p (i h) x"))
                if u == 2:
                    dve.wait_ge(small_in, 9 * 16)
                    step(nc.vector.tensor_scalar(rs_bc[:], rs_bc[:], 0.0, 0.3, ALU.max, ALU.min))
                if u == 3:
                    dve.wait_ge(od_saved, 2)
                    finite(clean_m[0:TT, 0:EARLY * H], n)
                if u == 4:
                    dve.wait_ge(bounds_ready, 9)
                    step(nc.vector.copy_predicated(d, clean_m[0:TT, 0:EARLY * H], n))
                    step(nc.vector.tensor_scalar(d, d, rs_bc[:, 0:1], None, ALU.mult))
                if u == 5:
                    moments(0, EARLY, delta)
                if u == 6:
                    add_delta(0, EARLY, 3)
                if u == 7:
                    moments(0, EARLY, x1)
                if u == 8:
                    normalise(0, EARLY, xn, x1, 4, xh_ready)
                if u == 10:
                    sigmoids(0, EARLY, 1)
                if u == 11:
                    group_bests(1, EARLY)

            def save_output(b):
                dve.wait_ge(pv_done, b * CH + CH)
                nc.vector.tensor_copy(o_all[:, :, b, :], PS[:, 7, 0:NT * S].rearrange("p (g s) -> p g s", g=NT)
                                      ).then_inc(o_saved, 1)

            def batch(b, last, beside=nothing, between=nothing, before_it=0):
                for m in range(PAIRS):
                    n = b * PAIRS + m
                    more = m + 1 < PAIRS or not last
                    clip(n * 2, 2 * m)
                    beside(before_it + m)
                    if more:
                        keys(n + 1, m + 1)
                        keys_lo(n + 1, m + 1)
                    clip(n * 2 + 1, 2 * m + 1)
                    if m + 2 < PAIRS or not last:
                        context_lo(n + 2, m + 2)
                    if more:
                        values(n + 1, m + 1)
                    if m == 0 and not (isinstance(b, int) and b == 0):
                        save_output(b - 1)
                    between(before_it + m)
                if last:
                    save_output(b)

            context_lo(0, 0)
            queries_saved(0, 1, first_pair, 1)
            nc.vector.memset(PS[:, 7, 0:NT * S], 0.0)
            clean(qT[:, :, 0:TT], q_raw[:, :, 0:TT], *(t[:, 0:KH * TT].rearrange("p (k c) -> p k c", k=KH)
                                                       for t in (clean_a, clean_m)))
            queries_split(0, 1)
            weight_lo(1)
            dve.wait_ge(pads_ready, 1)
            for half, group, to in ((0, 0, lower), (0, 0, upper), (0, 1, lower), (0, 1, upper), (1, 1, upper)):
                rows = (lower, upper)[group]
                if half == 1:
                    dve.wait_ge(qT_ready, 1)
                nc.vector.tensor_tensor(
                    q_bd[to, 0, half, :, group * HPG:(group + 1) * HPG],
                    (q_hi, q_lo)[half][rows, :, 0:S].bitcast(F32).unsqueeze(2).to_broadcast([GR, KH, HPG, S]),
                    head_mask[rows].unsqueeze(1).unsqueeze(3).to_broadcast([GR, KH, HPG, S]),
                    ALU.mult).then_inc(q_first_ready, 1)
                if (half, group, to) == (0, 1, upper):
                    keys(0, 0)
            keys_lo(0, 0)
            values(0, 0)
            context_lo(1, 1)

            batch(0, False, queries_beside, queries_between, 0)
            batch(1, False, queries_beside, queries_between, PAIRS)
            with dve.Fori(2, B - 2) as b:
                batch(b, False)
            batch(B - 2, False, rest_beside, rest_between, 0)
            batch(B - 1, True, rest_beside, rest_between, PAIRS)

            d, n = delta[:, EARLY], xn[:, EARLY]
            pick_groups(0, EARLY)
            dve.wait_ge(oT_psum, 3)
            attention_output(EARLY, NT, spare[0:TT, 0].rearrange("p (h x) -> p h x", x=SW))
            route_experts(0, EARLY)
            delta_saved(EARLY, NT, 2)
            dve.wait_ge(od_saved, 3)
            clean(d, n, clean_a[0:TT, 0:H], clean_m[0:TT, 0:H])
            step(nc.vector.tensor_scalar(d, d, rs_bc[:, 0:1], None, ALU.mult))
            moments(EARLY, NT, delta)
            add_delta(EARLY, NT, 5)
            moments(EARLY, NT, x1)
            normalise(EARLY, NT, xn, x1, 6, xh_ready)
            token_slots(0, EARLY, 1)
            dve.wait_ge(consts, 2)
            first_routes(0, EARLY, 0)
            sigmoids(EARLY, NT, 2)
            group_bests(EARLY, NT)
            pick_groups(EARLY, NT)
            route_experts(EARLY, NT)
            first_routes(0, EARLY, 1)
            token_slots(EARLY, NT, 2)
            def routes(q, c):
                g = q * QUAD + c
                after(dve, buf_psum, q * (QUAD // 2) + c // 2)
                after(dve, putb_ready, g - 1)
                nc.vector.tensor_tensor(
                    put[:, c % 2], slot_no[:].unsqueeze(1).unsqueeze(1).to_broadcast([TT, NT, GE, SLOT]),
                    slot[:, :, bass.ds(g * GE, GE)].unsqueeze(3).to_broadcast([TT, NT, GE, SLOT]),
                    ALU.is_equal).then_inc(put_ready, 1)

            def gathered(q, c):
                g = q * QUAD + c
                dve.wait_ge(buf_psum, q * (QUAD // 2) + c // 2 + 1)
                after(dve, gu_psum, g - 1)
                nc.vector.tensor_copy(bufT[:, c % 2, :, :, 0:CAP], buf_banks[:, :, c % 2]).then_inc(buf_ready, 1)

            def hidden(g, c):
                dve.wait_ge(actg_ready, g + 1)
                for e in range(2):
                    r = slice(e * SLOT, (e + 1) * SLOT)
                    nc.vector.tensor_reduce(slot_w[r, c % 2], sw_bank[r, :, e, :], AX.X, ALU.add).then_inc(sw_ready, 1)
                dve.wait_ge(sw_ready, g * 2 + 2)
                after(dve, hT_psum, g - 1)
                for p in range(2):
                    nc.vector.scalar_tensor_tensor(out=h_sb[:, c % 2, p], in0=act_g[:, c % 2, p],
                                                   scalar=slot_w[:, c % 2, p:p + 1], in1=gu_bank[:, p, 1, :],
                                                   op0=ALU.mult, op1=ALU.mult).then_inc(h_ready, 1)

            def outputs_lo(g, c):
                dve.wait_ge(z_saved, g * 3 + 3)
                after(dve, combined, (g - 1) * 2)
                nc.vector.tensor_tensor(eo_lo[:, c % 2], PS[:, 6 + (3 * c + 2) % 2, :].rearrange("p (k d) -> p k d", k=2),
                                        eo_hi[:, c % 2].bitcast(F32), ALU.subtract).then_inc(eo_ready, 1)

            def quad(q, last):
                for c in range(QUAD):
                    g = q * QUAD + c
                    hidden(g, c)
                    if c % 2 == 1 and (c + 1 < QUAD or not last):
                        gathered(q, c + 1)
                        gathered(q, c + 2)
                    if c + 3 < QUAD or not last:
                        routes(q, c + 3)
                    outputs_lo(g, c)

            dve.wait_ge(consts, 2)
            first_routes(EARLY, NT, 0)
            first_routes(EARLY, NT, 1)
            token_weights(0, NT, 2)
            dve.wait_ge(shg_ready, 1)
            nc.vector.tensor_tensor(sh_h, sh_g, PS[0:F, 4, 0:TOK], ALU.mult).then_inc(shh_ready, 1)
            gathered(0, 0)
            gathered(0, 1)
            weight_parts(0, NT, w3_ready)
            routes(0, 2)
            quad(0, False)
            with dve.Fori(1, GROUPS // QUAD - 1) as q:
                quad(q, False)
            quad(GROUPS // QUAD - 1, True)

            for i in range(2):
                dve.wait_ge(combined, (GROUPS - 1) * 2 + i + 1)
                nc.vector.tensor_tensor(y_sb[:, 2 * i:2 * i + 2], PS[0:TT, i, :].rearrange("p (i d) -> p i d", i=2),
                                        x1[:, 2 * i:2 * i + 2], ALU.add).then_inc(y_ready, 1)

        @block.tensor
        def _(pe):
            mm, turn = nc.tensor.matmul, nc.tensor.transpose

            def turn_weight(w):
                pe.wait_ge(w_in[w], 16)
                if w == 3:
                    pe.wait_ge(wT_ready, 1)
                for k in range(KH):
                    for o in range(KH):
                        ins = turn(PS[:, 3 + w % 3, k * H + o * 128:k * H + o * 128 + 128],
                                   w_raw[:, w, o, k * 128:k * 128 + 128], ident[:])
                ins.then_inc(wT_psum, 1)

            def turn_rows(i0, i1, src, banks, s):
                for k in range(KH):
                    for i in range(i0, i1):
                        ins = turn(banks[:, k, (i - i0) * TT:(i - i0 + 1) * TT], src[:, i, k * 128:(k + 1) * 128],
                                   ident[0:TT, 0:TT])
                ins.then_inc(s, 1)

            def queries(i0, i1, banks, count):
                pe.wait_ge(xT_ready, KH * count)
                for j in range(KH):
                    for k in range(KH):
                        ins = mm(banks[:, j, 0:(i1 - i0) * TT], wT[:, 0, k, j * 128:(j + 1) * 128],
                                 xT[:, k, i0 * TT:i1 * TT], start=(k == 0), stop=(k == KH - 1))
                ins.then_inc(q_psum, 1)

            def turn_output(tiles):
                for r, i in enumerate(tiles):
                    for g in range(NT):
                        ins = turn(spare[0:TT, r, g * 128:(g + 1) * 128],
                                   o_all[:, g, 2 * i:2 * i + 2, :].rearrange("p b s -> p (b s)"), ident[:])
                ins.then_inc(oT_psum, 1)

            def project_output(i0, i1, count):
                pe.wait_ge(aoT_ready, KH * count)
                for i in range(i0, i1):
                    r = i - i0
                    for k in range(KH):
                        ins = mm(spare[0:TT, r // 2, (r % 2) * H:(r % 2 + 1) * H], xT[:, k, i * TT:(i + 1) * TT],
                                 wT[:, 1, k, :], start=(k == 0), stop=(k == KH - 1))
                ins.then_inc(od_psum, 1)

            def logits(i0, i1, count):
                pe.wait_ge(xT_ready, KH * count)
                for i in range(i0, i1):
                    for k in range(KH):
                        ins = mm(PS[0:TT, 0, i * E:(i + 1) * E], xT[:, k, i * TT:(i + 1) * TT], gate_sb[:, k, :],
                                 start=(k == 0), stop=(k == KH - 1))
                ins.then_inc(logit_psum, 1)

            def turned(n, m, b):
                after(pe, cT_ready, n)
                if m % (CPP // 2) == 0:
                    pe.wait_ge(ctx_loaded[2 * m // CPP], (b + 1) * 16)
                for c in range(2):
                    ch = 2 * m + c
                    for k in range(KH):
                        ins = turn(turned_bank[:, k, c, :], ctx_sb[:, ch // CPP, ch % CPP, k * 128:(k + 1) * 128],
                                   ident[0:TP, 0:TP])
                ins.then_inc(cT_psum, 1)

            def project_keys(n, m):
                pe.wait_ge(cT_ready, n + 1)
                after(pe, k_raw, n)
                hi, lo = (t[:, m % 2].rearrange("p k c t -> p k (c t)") for t in (cT_hi, cT_lo))
                for j in range(KH):
                    js = slice(j * 128, (j + 1) * 128)
                    terms = [(w[:, 0, k, js], c[:, k, :]) for k in range(KH)
                             for w, c in ((wkv_hi, hi), (wkv_hi, lo), (wkv_lo, hi))]
                    for t, (w, c) in enumerate(terms):
                        ins = mm(key_bank[:, j, :], w, c, start=(t == 0), stop=(t == len(terms) - 1))
                ins.then_inc(k_psum, 1)

            def project_values(n, m):
                after(pe, v_ready, n)
                for c in range(2):
                    hi, lo = cT_hi[:, m % 2, :, c, 0:TP], cT_lo[:, m % 2, :, c, 0:TP]
                    terms = [(x[:, k, :], w[:, 1, k, :]) for k in range(KH)
                             for x, w in ((hi, wkv_hi), (hi, wkv_lo), (lo, wkv_hi))]
                    for t, (x, w) in enumerate(terms):
                        ins = mm(value_bank[:, c, :], x, w, start=(t == 0), stop=(t == len(terms) - 1))
                ins.then_inc(kv_psum, 1)

            def scores(n, c, b):
                after(pe, exp_done, n - 1)
                for j in range(KH):
                    for group in range(2):
                        heads = slice(group * HPG, (group + 1) * HPG)
                        for half in range(2):
                            ins = mm(score_banks(c)[:, j, group * HPG * S:(group + 1) * HPG * S],
                                     k_split[:, (c // 2) % 2, j, group, (c % 2) * TPE:(c % 2) * TPE + TP],
                                     q_bd[:, b % 2, half, j, heads].rearrange("p h s -> p (h s)"),
                                     start=(half == 0), stop=(half == 1))
                ins.then_inc(s_psum, 1)

            def weigh_values(n, m):
                pe.wait_ge(p_ready, n + 1)
                for h in range(NH):
                    i, g = h % NT, h // NT
                    ins = mm(PS[SW * i:SW * i + HD + 1, 7, g * S:(g + 1) * S], v_sb[:, m % 4, h, :],
                             p_sb[:, m % 3, h // HPH, (h % HPH) * S:(h % HPH + 1) * S],
                             start=(m == 0 and g == 0), stop=(m == CH - 1), skip_group_check=True)
                ins.then_inc(pv_done, 1)

            def nothing(u):
                pass

            def queries_beside(u):
                if u == 5:
                    pe.wait_ge(xh_ready, 2)
                    turn_rows(1, NT, xh, spare, xT_psum)
                if u == 6:
                    queries(1, NT, spare, 2)

            def queries_saved(u):
                if u == 5:
                    pe.wait_ge(xT_ready, KH * 2)
                if u == 6:
                    pe.wait_ge(q_saved, 2 * KH)

            def rest_beside(u):
                if u == 0:
                    turn_output((0, 1))
                if u == 1:
                    pe.wait_ge(o_saved, 2 * EARLY)
                    turn_output((2,))
                if u == 3:
                    project_output(0, EARLY, 1)
                if u == 9:
                    pe.wait_ge(xh_ready, 3)
                    turn_rows(0, EARLY, xn, spare, xT_psum)
                if u == 10:
                    pe.wait_ge(small_in, 9 * 16)
                    logits(0, EARLY, 3)

            def rest_midway(u):
                if u == 2:
                    pe.wait_ge(ao_ready, 2)
                    turn_rows(0, EARLY, ao, spare, aoT_psum)

            def rest_saved(u):
                if u in (0, 1):
                    pe.wait_ge(oT_saved, u + 2)
                if u == 2:
                    pe.wait_ge(aoT_ready, KH * 1)
                if u == 3:
                    pe.wait_ge(od_saved, 2)
                if u == 9:
                    pe.wait_ge(xT_ready, KH * 3)

            def batch(b, last, beside=nothing, midway=nothing, saved=nothing, before_it=0):
                first = isinstance(b, int) and b == 0
                if first:
                    pe.wait_ge(q_first_ready, 5)
                    pe.wait_ge(qbd_ready, 3)
                else:
                    pe.wait_ge(qbd_ready, b * 8 + 3)
                for m in range(PAIRS):
                    n = b * PAIRS + m
                    more = m + 1 < PAIRS or not last
                    pe.wait_ge(kT_ready, n * 2 + 2)
                    scores(n * 2, 2 * m, b)
                    if beside is not nothing:
                        pe.wait_ge(cT_ready, min(n + 2, B * PAIRS))
                        pe.wait_ge(v_ready, n + 1)
                    beside(before_it + m)
                    if more:
                        project_keys(n + 1, m + 1)
                    if m == 1:
                        after(pe, o_saved, b)
                    if m > 0 or not first:
                        weigh_values(n * 2 - 2, (2 * m - 2) % CH)
                    scores(n * 2 + 1, 2 * m + 1, b)
                    midway(before_it + m)
                    if m > 0 or not first:
                        weigh_values(n * 2 - 1, (2 * m - 1) % CH)
                    saved(before_it + m)
                    if m + 2 < PAIRS or not last:
                        turned(n + 2, (m + 2) % PAIRS, b + (m + 2) // PAIRS)
                    if more:
                        project_values(n + 1, m + 1)
                if last:
                    for c in range(CH - 2, CH):
                        weigh_values(b * CH + c, c)

            pe.wait_ge(ident_ready, 1)
            turn_weight(0)
            turn_weight(1)
            pe.wait_ge(xh_ready, 1)
            turn_rows(0, 1, xh, first_pair, xT_psum)
            turned(0, 0, 0)
            queries(0, 1, first_pair, 1)
            pe.wait_ge(w_lo_ready, 1)
            pe.wait_ge(pads_ready, 1)
            project_keys(0, 0)
            turn_weight(2)
            turned(1, 1, 0)
            turn_weight(3)
            pe.wait_ge(w_lo_ready, 2)
            project_values(0, 0)
            pe.wait_ge(wT_ready, 4)

            batch(0, False, queries_beside, nothing, queries_saved, 0)
            batch(1, False, queries_beside, nothing, queries_saved, PAIRS)
            with pe.Fori(2, B - 2) as b:
                batch(b, False)
            batch(B - 2, False, rest_beside, rest_midway, rest_saved, 0)
            batch(B - 1, True, rest_beside, rest_midway, rest_saved, PAIRS)

            pe.wait_ge(neg_ready, 1)
            pe.wait_ge(o_saved, B)
            turn_output((EARLY,))
            pe.wait_ge(ao_ready, 3)
            turn_rows(EARLY, NT, ao, spare, aoT_psum)
            project_output(EARLY, NT, 2)

            def shared(i0, i1):
                for u, w in enumerate((sg_sb, su_sb)):
                    for k in range(KH):
                        ins = mm(PS[0:F, 3 + u, i0 * TT:i1 * TT], w[:, k, :], xT[:, k, i0 * TT:i1 * TT],
                                 start=(k == 0), stop=(k == KH - 1))
                ins.then_inc(sh_psum, 1)

            def positions(i0, i1, count):
                pe.wait_ge(consts, 2)
                for i in range(i0, i1):
                    for j in range(i + 1):
                        if j == i0:
                            pe.wait_ge(pick_ready, count)
                        ins = mm(PS[0:TT, 7 - i // EARLY, i * E:(i + 1) * E], before[:] if j == i else ones[:], pick[:, j, :],
                                 start=(j == 0), stop=(j == i))
                ins.then_inc(pos_psum, 1)

            positions(0, EARLY, 1)
            shared(0, EARLY)
            pe.wait_ge(xh_ready, 4)
            turn_rows(EARLY, NT, xn, spare, xT_psum)
            logits(EARLY, NT, 4)
            shared(EARLY, NT)
            positions(EARLY, NT, 2)
            def gather(g):
                pe.wait_ge(put_ready, g + 2)
                after(pe, buf_ready, g)
                for k in range(KH):
                    for i in range(NT):
                        for part in (xn_hi, xn_lo):
                            ins = mm(PS[:, 2 + k, 0:2 * GE * CAP], part[:, i, k:H:KH], put[:, :, i, :, 0:CAP],
                                     start=(i == 0 and part is xn_hi), stop=(i == NT - 1 and part is xn_lo))
                ins.then_inc(buf_psum, 1)

            def gate_up(g, c, q):
                pe.wait_ge(buf_ready, g + 1)
                pe.wait_ge(ew_loaded[c], (q + 1) * 48)
                after(pe, h_ready, g * 2)
                for p in range(2):
                    for k in range(KH):
                        for e in range(2):
                            mm(gu_bank[e * SLOT:(e + 1) * SLOT, p], bufT[:, c % 2, k, 2 * p + e, :],
                               wgu_sb[:, c, 2 * p + e, :, k, :], start=(k == 0), stop=(k == KH - 1), skip_group_check=True)
                pe.wait_ge(putb_ready, g + 1)
                if isinstance(g, int) and g == 0:
                    pe.wait_ge(w3_ready, 1)
                for p in range(2):
                    for i in range(NT):
                        ins = mm(sw_bank[:, p].rearrange("p e w -> p (e w)"), put_b[:, c % 2, i, 2 * p * SLOT:2 * (p + 1) * SLOT],
                                 w3[:, i, bass.ds(g * GE + 2 * p, 2), :].rearrange("p e w -> p (e w)"),
                                 start=(i == 0), stop=(i == NT - 1), skip_group_check=True)
                ins.then_inc(gu_psum, 1)

            def turn_put(g, c):
                for p in range(2):
                    if p == 0:
                        after(pe, z_saved, g * 3 - 1)
                    else:
                        after(pe, eo_ready, g)
                    for i in range(NT):
                        ins = turn(PS[:, 6 + (3 * c + p) % 2, :].bitcast(BF16)[:, i * TT:(i + 1) * TT],
                                   put_b[:, c % 2, i, 2 * p * SLOT:2 * (p + 1) * SLOT], ident_b[0:TT, 0:TT])
                    ins.then_inc(z_psum, 1)

            def turn_hidden(g, c):
                pe.wait_ge(h_ready, g * 2 + 2)
                after(pe, hT_ready, g)
                for p in range(2):
                    ins = turn(hT_bank[:, p * 128:(p + 1) * 128], h_sb[:, c % 2, p], ident[:])
                ins.then_inc(hT_psum, 1)

            def down(g, c):
                pe.wait_ge(hT_ready, g + 1)
                pe.wait_ge(z_saved, g * 3 + 1)
                for e in range(GE):
                    r = SLOT * (e % 2)
                    ins = mm(PS[r:r + SLOT, 6 + (3 * c + 2) % 2, (e // 2) * H:(e // 2 + 1) * H],
                             hT[:, c % 2, e * SLOT:(e + 1) * SLOT], wd_sb[:, c, e, :],
                             start=True, stop=True, skip_group_check=True)
                ins.then_inc(z_psum, 1)

            def combine(g, c, halves=(0, 1)):
                pe.wait_ge(eo_ready, g + 1)
                for p in halves:
                    for i in range(NT):
                        for part in (eo_hi, eo_lo):
                            ins = mm(y_bank(i), putT[:, c % 2, p, i * TT:(i + 1) * TT], part[:, c % 2, p, :],
                                     start=False, stop=True, skip_group_check=True)
                    ins.then_inc(combined, 1)

            def quad(q, first, last):
                for c in range(QUAD):
                    g = q * QUAD + c
                    gate_up(g, c, q)
                    turn_put(g, c)
                    if c % 2 == 1 and (c + 1 < QUAD or not last):
                        gather(g + 1)
                    split = c % 2 == 0 or (last and c == QUAD - 1)
                    if split and (c > 0 or not first):
                        combine(g - 1, c + 1, (0,))
                    turn_hidden(g, c)
                    if c > 0 or not first:
                        combine(g - 1, c + 1, (1,) if split else (0, 1))
                    down(g, c)

            pe.wait_ge(xs_ready, 2)
            pe.wait_ge(shg_ready, 1)
            pe.wait_ge(put_early_ready, 2)
            gather(0)
            pe.wait_ge(shh_ready, 1)
            for i in range(NT):
                mm(y_bank(i), sh_h[:, i * TT:(i + 1) * TT], sd_sb[:], start=(i % 2 == 0), stop=False, skip_group_check=True)

            quad(0, True, False)
            with pe.Fori(1, GROUPS // QUAD - 1) as q:
                quad(q, False, False)
            quad(GROUPS // QUAD - 1, False, True)
            pe.wait_ge(eo_ready, GROUPS)
            for i in range(NT):
                for p in range(2):
                    for part in (eo_hi, eo_lo):
                        ins = mm(y_bank(i), putT[:, (GROUPS - 1) % 2, p, i * TT:(i + 1) * TT], part[:, (GROUPS - 1) % 2, p, :],
                                 start=False, stop=True, skip_group_check=True)
                if i % 2 == 1:
                    ins.then_inc(combined, 1)


_INS = ["x", "ctx_2048", "mask_BxS2_ik0", "L0_xattn_Wq", "L0_xattn_bq", "L0_xattn_Wk", "L0_xattn_bk", "L0_xattn_Wv",
        "L0_xattn_bv", "L0_xattn_Wo", "L0_xattn_bo", "L0_xattn_ln_gamma", "L0_xattn_ln_beta",
        "L0_xattn_residual_scale", "L0_ffn_gate_w", "L0_ffn_bias", "L0_ffn_w_gate", "L0_ffn_w_up", "L0_ffn_w_down",
        "L0_ffn_ws_gate", "L0_ffn_ws_up", "L0_ffn_ws_down"]


def kernel(**inputs):
    import numpy as np
    import concourse.bacc as bacc
    from concourse.bass_utils import run_bass_kernel_spmd

    nc = bacc.Bacc("TRN2", target_bir_lowering=False, num_devices=1)
    arrays, args = {}, []
    for name in _INS:
        a = np.ascontiguousarray(inputs[name])
        if a.ndim == 0:
            a = a.reshape(1)
        arrays[f"in_{name}"] = a
        args.append(nc.dram_tensor(f"in_{name}", a.shape, mybir.dt.from_np(a.dtype), kind="ExternalInput").ap())
    args.append(nc.dram_tensor("out_0", (B, S, H), F32, kind="ExternalOutput").ap())
    build(nc, *args)
    r = run_bass_kernel_spmd(nc, [arrays], core_ids=[0])
    return r.results[0]["out_0"]
```
